# Optimizing a Trainium2 kernel written in Bass

```python
import numpy as np
import jax
import jax.numpy as jnp

def _softmax(x, axis=-1):
    return jax.nn.softmax(x, axis=axis)

def _gelu(x):
    return jax.nn.gelu(x, approximate=True)

def _silu(x):
    return jax.nn.silu(x)

def _sigmoid(x):
    return jax.nn.sigmoid(x)

def _layernorm(x, axis=-1, eps=1e-05):
    m = jnp.mean(x, axis=axis, keepdims=True)
    v = jnp.var(x, axis=axis, keepdims=True)
    return (x - m) / jnp.sqrt(v + eps)

def _scatter_add(tgt, idx, src, axis=0):
    return tgt.at[idx].add(src)

def _segment_sum(src, seg, n):
    return jax.ops.segment_sum(src, seg, n)
kernel_name = 'mk_adj_preln_d2_adj_r2_877886'

def setup_inputs(seed: int=0):
    np.random.seed(seed)
    _w = jnp.asarray

    def _rec_inputs():
        import jax
        import jax.numpy as jnp
        _gk = jax.random.key(seed)
        x = -0.0005207 + 1.001 * jax.random.normal(jax.random.fold_in(_gk, 1), (4096, 128), jnp.float32)
        _a = jax.random.bernoulli(jax.random.fold_in(_gk, 2), 0.00390625, (4096, 4096))
        adj = _a.astype(jnp.int32)
        return (x, adj)
    x, adj = _rec_inputs()

    def _L0_gnn_setup():
        import jax, jax.numpy as jnp
        import numpy as np
        N, D, H = (4096, 128, 128)
        NEG_BIG = -1000000000.0
        LEAKY_SLOPE = 0.01
        key = jax.random.key(seed)
        ks = jax.random.split(key, 6)
        inlayer = jax.random.normal(ks[0], (N, D), jnp.float32)
        inlayer2 = jax.random.normal(ks[1], (N, D), jnp.float32)
        adj_mat = jax.random.randint(ks[2], (N, N), 0, 2, jnp.int32)
        W = jax.random.uniform(ks[3], (H, D), jnp.float32, -1.0, 1.0) * np.float32(np.sqrt(6.0 / (D + H)))
        b = jnp.zeros((H,), jnp.float32)
        w1 = jax.random.uniform(ks[4], (H,), jnp.float32, -1.0, 1.0) * np.float32(np.sqrt(6.0 / (H + 1)))
        b1 = jnp.zeros((1,), jnp.float32)
        w2 = jax.random.uniform(ks[5], (H,), jnp.float32, -1.0, 1.0) * np.float32(np.sqrt(6.0 / (H + 1)))
        b2 = jnp.zeros((1,), jnp.float32)
        return {'inlayer': inlayer, 'inlayer2': inlayer2, 'adj_mat': adj_mat, 'W': W, 'b': b, 'w1': w1, 'b1': b1, 'w2': w2, 'b2': b2}
    _L0_gnn_all = _L0_gnn_setup()
    _L0_gnn_in = {k: v for k, v in _L0_gnn_all.items() if k in ('inlayer2', 'W', 'b', 'w1', 'b1', 'w2', 'b2')}
    del _L0_gnn_all

    def _L1_gnn_setup():
        import jax, jax.numpy as jnp
        import numpy as np
        N, IN_DIM, OUT_DIM, HEADS = (4096, 128, 128, 2)
        C = OUT_DIM // HEADS
        ALPHA = 0.2
        NEG = -9000000000000000.0
        key = jax.random.key(seed)
        ks = jax.random.split(key, 9)
        h = jax.random.normal(ks[0], (N, IN_DIM), dtype=jnp.float32)
        adj = jax.random.randint(ks[1], (N, N), 0, 2, dtype=jnp.int32)

        def xav(k, shape):
            fan_in, fan_out = (shape[1], shape[0])
            s = 1.414 * np.sqrt(6.0 / (fan_in + fan_out))
            return jax.random.uniform(k, shape, jnp.float32, -s, s)
        W1 = xav(ks[2], (HEADS * C, IN_DIM))
        W2 = xav(ks[3], (HEADS * C, IN_DIM))
        W3 = xav(ks[4], (HEADS * C, IN_DIM))
        b1 = jnp.zeros((HEADS * C,), jnp.float32)
        b2 = jnp.zeros((HEADS * C,), jnp.float32)
        b3 = jnp.zeros((HEADS * C,), jnp.float32)
        sa = 1.414 * np.sqrt(6.0 / (HEADS + 2 * C))
        a = jax.random.uniform(ks[5], (HEADS, 2 * C), jnp.float32, -sa, sa)
        return {'h': h, 'adj': adj, 'W1': W1, 'b1': b1, 'W2': W2, 'b2': b2, 'W3': W3, 'b3': b3, 'a': a}
    _L1_gnn_all = _L1_gnn_setup()
    _L1_gnn_in = {k: v for k, v in _L1_gnn_all.items() if k in ('W1', 'b1', 'W2', 'b2', 'W3', 'b3', 'a')}
    del _L1_gnn_all
    return {'x': x, 'adj': adj, 'L0_gnn_inlayer2': _L0_gnn_in['inlayer2'], 'L0_gnn_W': _L0_gnn_in['W'], 'L0_gnn_b': _L0_gnn_in['b'], 'L0_gnn_w1': _L0_gnn_in['w1'], 'L0_gnn_b1': _L0_gnn_in['b1'], 'L0_gnn_w2': _L0_gnn_in['w2'], 'L0_gnn_b2': _L0_gnn_in['b2'], 'L1_gnn_W1': _L1_gnn_in['W1'], 'L1_gnn_b1': _L1_gnn_in['b1'], 'L1_gnn_W2': _L1_gnn_in['W2'], 'L1_gnn_b2': _L1_gnn_in['b2'], 'L1_gnn_W3': _L1_gnn_in['W3'], 'L1_gnn_b3': _L1_gnn_in['b3'], 'L1_gnn_a': _L1_gnn_in['a']}

def reference(x, adj, L0_gnn_inlayer2, L0_gnn_W, L0_gnn_b, L0_gnn_w1, L0_gnn_b1, L0_gnn_w2, L0_gnn_b2, L1_gnn_W1, L1_gnn_b1, L1_gnn_W2, L1_gnn_b2, L1_gnn_W3, L1_gnn_b3, L1_gnn_a):
    import jax
    import jax.numpy as jnp

    def _L0_gnn_ref(inlayer, inlayer2, adj_mat, W, b, w1, b1, w2, b2):
        import jax, jax.numpy as jnp
        import numpy as np
        N, D, H = (4096, 128, 128)
        NEG_BIG = -1000000000.0
        LEAKY_SLOPE = 0.01
        h = inlayer2 @ W.T + b
        f1 = h @ w1 + b1
        f2 = h @ w2 + b2
        logits = f1[:, None] + f2[None, :]
        bias_mat = NEG_BIG * (1.0 - (adj_mat > 0).astype(jnp.float32))
        coefs = jax.nn.softmax(jax.nn.leaky_relu(logits, LEAKY_SLOPE) + bias_mat, axis=-1)
        vals = coefs @ inlayer
        return vals

    def _L1_gnn_ref(h, adj, W1, b1, W2, b2, W3, b3, a):
        import jax, jax.numpy as jnp
        import numpy as np
        N, IN_DIM, OUT_DIM, HEADS = (4096, 128, 128, 2)
        C = OUT_DIM // HEADS
        ALPHA = 0.2
        NEG = -9000000000000000.0
        n = h.shape[0]
        W1h = (h @ W1.T + b1).reshape(n, HEADS, C)
        W2h = (h @ W2.T + b2).reshape(n, HEADS, C)
        W3h = (h @ W3.T + b3).reshape(n, HEADS, C)
        a1, a2 = (a[:, :C], a[:, C:])
        s1 = jnp.einsum('nhc,hc->nh', W1h, a1)
        s2 = jnp.einsum('nhc,hc->nh', W2h, a2)
        e = jax.nn.leaky_relu(s1[:, None, :] + s2[None, :, :], ALPHA)
        e = jnp.where(adj[:, :, None] == 1, e, NEG)
        att = jax.nn.softmax(e, axis=1)
        h_prime = jnp.einsum('ijh,jhc->ihc', att, W3h)
        return h_prime.reshape(n, HEADS * C)
    h = jnp.maximum(_layernorm(x, axis=-1), 0.0)
    x = x + _L0_gnn_ref(h, L0_gnn_inlayer2, adj, L0_gnn_W, L0_gnn_b, L0_gnn_w1, L0_gnn_b1, L0_gnn_w2, L0_gnn_b2)
    h = jnp.maximum(_layernorm(x, axis=-1), 0.0)
    x = x + _L1_gnn_ref(h, adj, L1_gnn_W1, L1_gnn_b1, L1_gnn_W2, L1_gnn_b2, L1_gnn_W3, L1_gnn_b3, L1_gnn_a)
    return x

_drawn_inputs = setup_inputs


def setup_inputs(seed=0):
    import zlib

    import numpy as np

    out = dict(_drawn_inputs(seed))
    spreads = {'L0_gnn_b': (0.0, 0.507),
     'L1_gnn_b1': (0.0, 0.8),
     'L1_gnn_b2': (0.0, 0.8),
     'L1_gnn_b3': (0.0, 0.1)}
    factors = {}
    for name, (base, spread) in spreads.items():
        noise = np.random.default_rng([zlib.crc32(name.encode()), seed]).standard_normal(out[name].shape)
        drawn = base * np.exp(spread * noise) if base else spread * noise
        out[name] = jnp.asarray(drawn.astype(out[name].dtype))
    for name, factor in factors.items():
        out[name] = (out[name] * factor).astype(out[name].dtype)
    return out
```

```python
import concourse.bass as bass
from concourse import mybir
from concourse.alu_op_type import AluOpType as ALU
from contextlib import ExitStack

F32 = mybir.dt.float32
F16 = mybir.dt.float16
BF16 = mybir.dt.bfloat16
I32 = mybir.dt.int32
ACT = mybir.ActivationFunctionType
AX = mybir.AxisListType
RMAX = bass.bass_isa.ReduceOp.max
RADD = bass.bass_isa.ReduceOp.add

N = 4096
D = 128
P = 128
T = N // P
IB = 512
NB = N // IB
KT = IB // P
G = 4
NG = T // G
RAW = 4
LO = 2.0 ** 11
WSC = 2.0 ** 11
EPS = 1e-5
SPREAD = 16.0
LOGIT = 30.0
VMAX = 31.0


def gat_program(nc, x_d, adjT_d, adj_d, x2T_d, W_d, b_d, w12_d, b12_d,
                W1_d, W2_d, W3T_d, pb1_d, pb2_d, pb3_d, a_d, out_d):
    ctx = ExitStack()
    with ctx:
        def sb(name, shape, dt=F32):
            return ctx.enter_context(nc.sbuf_tensor(name, shape, dt))

        def sem(name):
            return ctx.enter_context(nc.semaphore(name))

        x = sb("x", [P, T, D])
        featT = sb("featT", [P, N])
        f1bc0 = sb("f1bc0", [P, N])
        f1bc = (f1bc0, featT)
        raw = sb("raw", [P, RAW, G * IB], I32)
        q = sb("q", [P, 2, G * IB], BF16)
        s = sb("s", [P, 2, 2, G * IB], BF16)
        bc = sb("bc", [P, 2, 2, 2, G * IB], BF16)
        vals = sb("vals", [P, T, 130])
        h = vals[:, :, 0:D]
        xy = sb("xy", [P, T, 520], F16)
        tb = sb("tb", [P, KT, 260])
        acc = sb("acc", [P, KT, 260])
        prod = tb[:, :, :].rearrange("p (k t) w -> p k (t w)", k=2)
        diff = acc[:, :, :].rearrange("p (k t) w -> p k (t w)", k=2)
        comb = sb("comb", [P, KT, 130])
        fix = sb("fix", [P, KT, 130])
        vsum = sb("vsum", [P, 130])
        vpart = sb("vpart", [P, 130])
        ones = sb("ones", [P, P])
        ident = sb("ident", [P, P])
        early = bc[:, 0, 0, :, :].rearrange("p h i -> p (h i)").bitcast(F32)
        W, W1, W2 = (early[:, r * D:(r + 1) * D] for r in range(3))
        bb = early[:, 3 * D:6 * D].rearrange("p (r m) -> p r m", r=3)
        bcols = sb("bcols", [P, 3])
        w12 = sb("w12", [P, 2])
        A = sb("A", [P, 4])
        b12 = sb("b12", [P, 2])
        b3 = sb("b3", [P, D])
        pv = sb("pv", [P, 6])
        pc = sb("pc", [P, 6])
        pvb = sb("pvb", [P, 3, P])
        rhs1 = sb("rhs1", [P, D + 4])
        fc = sb("fc", [P, T, 4])
        nfc = sb("nfc", [P, T, 4])
        four = sb("four", [P, 2])
        E = sb("E", [P, 2, T, 2])
        uv = sb("uv", [P, T, 2, 2])
        uvt = sb("uvt", [P, 4, T, 2])
        uvcur = sb("uvcur", [P, KT, 2, 2])
        st = sb("st", [P, 10])
        sta = sb("sta", [P, 10])
        ng = sb("ng", [P, 4])
        flagf = sb("flagf", [P, 12])
        nz = sb("nz", [P, KT, 2])
        rden = sb("rden", [P, KT, 2])
        bst = sb("bst", [P, KT, 6])
        bag = sb("bag", [P, KT, 2])
        vare = sb("vare", [P, KT])
        pause = sb("pause", [P, 1])
        flag = sb("flag", [P, 2], I32)
        am = sb("am", [P, 4])
        ok = sb("ok", [P, 8])
        nmax = sb("nmax", [P, 1])
        rsum = sb("rsum", [P, 2])
        gadj = bc[:, 0, :, :, :].rearrange("p k h i -> p (k h i)").bitcast(I32)[:, 0:N]
        gneg = bc[:, 0, :, :, :].rearrange("p k h i -> p (k h i)").bitcast(F32)[:, 0:N]
        glog = bc[:, 1, :, :, :].rearrange("p k h i -> p (k h i)").bitcast(F32)[:, 0:N]
        gT = s[:, :, :, :].rearrange("p k h i -> p (k h i)").bitcast(F32)[:, 0:N]
        gf2 = xy[:, :, :].rearrange("p t w -> p (t w)").bitcast(F32)[:, 0:N]
        gcol = fix[:, :, :].rearrange("p k w -> p (k w)")[:, 0:P]
        mhalf = sb("mhalf", [P, KT])
        rstd = sb("rstd", [P, KT])

        bank = [ctx.enter_context(nc.psum_tensor(f"bank{i}", [P, 512], F32)) for i in range(8)]

        LAY = [dict(i=0, H=1, Wd=129, slope=0.01, logit=LOGIT), dict(i=1, H=2, Wd=65, slope=0.2, logit=1e30)]
        for L in LAY:
            i = L["i"]
            L["adj_in"] = [sem(f"adj_in{i}_{r}") for r in range(RAW)]
            for name in ("q_ready", "s_ready", "t_ready", "g_ready", "bc_ready", "bc_used", "tiles_done",
                         "uv_ready", "b_scaled", "banks_free", "comb_done", "nz_done", "fix_done", "sum_done",
                         "rden_done", "x_done", "stat", "allmax", "g_max", "exp_done", "uvp", "uv_set", "e_ready",
                         "flag_ready", "gen_adj_in", "gen_col", "gen_mm", "gen_row", "gen_logit", "gen_exp", "gen_tr",
                         "gen_pt", "gen_sum", "gen_rec", "gen_free", "gen_step",
                         "x_prod", "hi_done", "d_done", "xy_ready", "vpart_done", "vsum_ready"):
                L[name] = sem(f"{name}{i}")
        for ln in ("ln0", "ln1"):
            LAY[0][ln] = {name: sem(f"{ln}_{name}") for name in ("bst_done", "bag_done", "var_done", "rstd_done", "norm_done", "h_done")}
        x_in = [sem(f"x_in{c}") for c in range(4)]
        feat_in = [sem(f"feat_in{c}") for c in range(4)]
        consts_in = sem("consts_in")
        A_in = sem("A_in")
        ident0 = sem("ident0")
        bb_ready = sem("bb_ready")
        pv_mm = sem("pv_mm")
        pv_ready = sem("pv_ready")
        fcol_mm = sem("fcol_mm")
        fbc_mm = sem("fbc_mm")
        fbc_ready = sem("fbc_ready")
        fc_ready = sem("fc_ready")
        trans_mm = sem("trans_mm")
        hT_ready = sem("hT_ready")
        v_mm = sem("v_mm")
        v_ready = sem("v_ready")
        dve_step = sem("dve_step")
        out_done = sem("out_done")

        x_t = x_d.rearrange("(t p) d -> p t d", p=P)
        out_t = out_d.rearrange("(t p) d -> p t d", p=P)
        adjT_t = adjT_d.rearrange("(t p) i -> p t i", p=P)

        def xy5(L):
            return xy[:, :, 0:4 * L["H"] * L["Wd"]].rearrange("p t (k h r w) -> p t k h r w", k=2, h=L["H"], r=2)

        def vals3(L):
            return vals[:, :, 0:L["H"] * L["Wd"]].rearrange("p t (h w) -> p t h w", h=L["H"])

        def load_unit(sp, L, b, g, first):
            if not first:
                sp.wait_ge(L["q_ready"], NG * b + g - RAW + 1)
            sp.dma_start(raw[:, g % RAW, :].rearrange("p (t i) -> p t i", t=G),
                         adjT_t[:, G * g:G * g + G, bass.ds(b * IB, IB)]).then_inc(L["adj_in"][g % RAW], 16)

        def act_jts(L, g):
            if L["i"] == 0:
                return [(j, 0) for j in range(3)]
            return [(j, hh) for hh in range(2) for j in range(4) if not (hh == 1 and j >= 2)]

        def dve_jts(L, g):
            return [(j, hh) for hh in range(L["H"]) for j in range(G) if (j, hh) not in act_jts(L, g)]

        def scalar_unit(act, L, b, g, first=False):
            n = NG * b + g
            if g >= 2 or not first:
                act.wait_ge(L["bc_ready"], n - 1)
            act.wait_ge(L["adj_in"][g % RAW], 16 * (2 * b + g // RAW + 1))
            if L["i"] == 0:
                nc.scalar.activation(q[:, g % 2, :], raw[:, g % RAW, :], ACT.Relu, bias=four[:, 0:1],
                                     scale=-4.0).then_inc(L["q_ready"], 1)
            else:
                nc.scalar.activation(q[:, g % 2, :], raw[:, g % RAW, :], ACT.Square, bias=four[:, 1:2],
                                     scale=2.0).then_inc(L["q_ready"], 1)
            for j, hh in act_jts(L, g):
                last = nc.scalar.activation(s[:, g % 2, hh, j * IB:(j + 1) * IB], f1bc[hh][:, bass.ds(b * IB, IB)],
                                            ACT.Sign, bias=nfc[:, G * g + j, L["H"] + hh:L["H"] + hh + 1], scale=-1.0)
            last.then_inc(L["s_ready"], 1)

        def vector_unit(dve, L, b, g, first=False):
            n = NG * b + g
            H = L["H"]
            for j, hh in dve_jts(L, g):
                last = nc.vector.tensor_scalar(s[:, g % 2, hh, j * IB:(j + 1) * IB], f1bc[hh][:, bass.ds(b * IB, IB)],
                                               nfc[:, G * g + j, L["H"] + hh:L["H"] + hh + 1], None, ALU.is_lt)
            last.then_inc(L["t_ready"], 1)
            dve.wait_ge(L["q_ready"], n + 1)
            dve.wait_ge(L["s_ready"], n + 1)
            dve.wait_ge(L["t_ready"], n + 1)
            for hh in range(H):
                last = nc.vector.tensor_tensor(s[:, g % 2, hh, :], s[:, g % 2, hh, :], q[:, g % 2, :], ALU.add)
            last.then_inc(L["g_ready"], 1)
            dve.wait_ge(L["g_ready"], n + 1)
            if g >= 2:
                dve.wait_ge(L["bc_used"], (NG - 1) * b + g - 1)
            elif g == 1 and not first:
                dve.wait_ge(L["tiles_done"], KT * b)
            elif not first:
                dve.wait_ge(L["bc_used"], (NG - 1) * b)
            nc.vector.tensor_scalar(bc[:, g % 2, 0, 0:H, :], s[:, g % 2, 0:H, :], 0.0, None, ALU.is_le)
            nc.vector.tensor_scalar(bc[:, g % 2, 1, 0:H, :], s[:, g % 2, 0:H, :], 1.0, None,
                                    ALU.is_equal).then_inc(L["bc_ready"], 1)

        def tensor_unit(pe, L, b, g, first):
            H, Wd = L["H"], L["Wd"]
            v = xy5(L)
            if first:
                pe.wait_ge(L["xy_ready"], 2 * (g + 1))
            pe.wait_ge(L["bc_ready"], NG * b + g + 1)
            for k in range(KT):
                if g == 0 and not first:
                    pe.wait_ge(L["banks_free"], KT * b - KT + k + 1)
                for j in range(G):
                    for kind in range(2):
                        for hh in range(H):
                            mm = nc.tensor.matmul(bank[2 * k + kind][:, hh * 2 * Wd:(hh + 1) * 2 * Wd],
                                                  bc[:, g % 2, kind, hh, j * IB + k * P:j * IB + (k + 1) * P],
                                                  v[:, G * g + j, kind, hh, :, :],
                                                  start=(g == 0 and j == 0 and hh == 0), stop=(g == NG - 1 and j == G - 1),
                                                  skip_group_check=True)
                if g == NG - 1:
                    mm.then_inc(L["tiles_done"], 1)
            if g < NG - 1:
                mm.then_inc(L["bc_used"], 1)

        def tensor_core(pe, L):
            for g in range(NG):
                tensor_unit(pe, L, 0, g, True)
            with pe.Fori(1, NB) as b:
                for g in range(NG):
                    tensor_unit(pe, L, b, g, False)

        def scalar_evac(act, L, b):
            H, Wd = L["H"], L["Wd"]
            act.wait_ge(L["uv_ready"], b + 1)
            for k in range(KT):
                act.wait_ge(L["tiles_done"], KT * b + k + 1)
                for hh in range(H):
                    c = slice(hh * 2 * Wd, (hh + 1) * 2 * Wd)
                    last = nc.scalar.activation(tb[:, k, c], bank[2 * k][:, c], ACT.Copy, scale=uvcur[:, k, 0, hh:hh + 1])
                last.then_inc(L["b_scaled"], 1)

        def vector_evac(dve, L, b):
            H, Wd = L["H"], L["Wd"]
            CW = H * Wd
            nc.vector.tensor_scalar(uvcur[:, :, :, 0:H], uv[:, bass.ds(b * KT, KT), :, 0:H], 1.0, None,
                                    ALU.mult).then_inc(L["uv_ready"], 1)
            dve.wait_ge(L["uv_ready"], b + 1)
            for k in range(KT):
                dve.wait_ge(L["b_scaled"], KT * b + k + 1)
                for hh in range(H):
                    c = slice(hh * 2 * Wd, (hh + 1) * 2 * Wd)
                    last = nc.vector.scalar_tensor_tensor(out=acc[:, k, c], in0=bank[2 * k + 1][:, c],
                                                          scalar=uvcur[:, k, 1, hh:hh + 1], in1=tb[:, k, c],
                                                          op0=ALU.mult, op1=ALU.add)
                last.then_inc(L["banks_free"], 1)
            dve.wait_ge(L["banks_free"], KT * b + KT)
            for k in range(KT):
                a4 = acc[:, k, 0:2 * CW].rearrange("p (h r w) -> p h r w", h=H, r=2)
                last = nc.vector.scalar_tensor_tensor(out=comb[:, k, 0:CW].rearrange("p (h w) -> p h w", h=H),
                                                      in0=a4[:, :, 1, :], scalar=1.0 / LO, in1=a4[:, :, 0, :],
                                                      op0=ALU.mult, op1=ALU.add)
            last.then_inc(L["comb_done"], 1)
            dve.wait_ge(L["comb_done"], b + 1)
            c4 = comb[:, :, 0:CW].rearrange("p k (h w) -> p k h w", h=H)
            f4 = fix[:, :, 0:CW].rearrange("p k (h w) -> p k h w", h=H)
            nc.vector.tensor_scalar(nz[:, :, 0:H], c4[:, :, :, Wd - 1], 0.0, None, ALU.is_equal).then_inc(L["nz_done"], 1)
            dve.wait_ge(L["nz_done"], b + 1)
            vs = vsum[:, 0:CW].rearrange("p (o h w) -> p o h w", o=1, h=H).broadcast_to([P, KT, H, Wd])
            nc.vector.tensor_tensor(f4, vs, nz[:, :, 0:H].unsqueeze(3).broadcast_to([P, KT, H, Wd]),
                                    ALU.mult).then_inc(L["fix_done"], 1)
            dve.wait_ge(L["fix_done"], b + 1)
            nc.vector.tensor_tensor(fix[:, :, 0:CW], comb[:, :, 0:CW], fix[:, :, 0:CW], ALU.add).then_inc(L["sum_done"], 1)
            dve.wait_ge(L["sum_done"], b + 1)
            nc.vector.reciprocal(rden[:, :, 0:H], f4[:, :, :, Wd - 1]).then_inc(L["rden_done"], 1)
            dve.wait_ge(L["rden_done"], b + 1)
            for k in range(KT):
                for hh in range(H):
                    w = Wd - 1
                    xs = x[:, bass.ds(b * KT + k, 1), hh * w:(hh + 1) * w].rearrange("p o w -> p (o w)")
                    last = nc.vector.scalar_tensor_tensor(out=xs, in0=f4[:, k, hh, 0:w], scalar=rden[:, k, hh:hh + 1],
                                                          in1=xs, op0=ALU.mult, op1=ALU.add)
            last.then_inc(L["x_done"], 1)

        def layernorm(dve, L, b, dst):
            for k in range(KT):
                last = nc.vector.bn_stats(bst[:, k, :], x[:, bass.ds(b * KT + k, 1), :].rearrange("p o w -> p (o w)"))
            last.then_inc(L["bst_done"], 1)
            dve.wait_ge(L["bst_done"], b + 1)
            nc.vector.memset(pause[:, :], 0.0)
            for k in range(KT):
                last = nc.vector.bn_aggr(bag[:, k, :], bst[:, k, :])
            last.then_inc(L["bag_done"], 1)
            dve.wait_ge(L["bag_done"], b + 1)
            nc.vector.tensor_scalar(vare[:, :], bag[:, :, 1], EPS, None, ALU.add).then_inc(L["var_done"], 1)
            dve.wait_ge(L["rstd_done"], b + 1)
            for k in range(KT):
                last = nc.vector.tensor_scalar(dst(b, k, 1), x[:, bass.ds(b * KT + k, 1), :],
                                               bag[:, k, 0:1], rstd[:, k:k + 1], ALU.subtract, ALU.mult)
            last.then_inc(L["norm_done"], 1)
            dve.wait_ge(L["norm_done"], b + 1)
            nc.vector.tensor_scalar(dst(b, 0, KT), dst(b, 0, KT), 0.0, None, ALU.max).then_inc(L["h_done"], 1)

        def pool_rstd(pool, L, b):
            pool.wait_ge(L["var_done"], b + 1)
            nc.gpsimd.tensor_tensor(rstd[:, :], vare[:, :], mhalf[:, :], ALU.pow).then_inc(L["rstd_done"], 1)

        def run_core(eng, pre, unit, between, after):
            for g in range(NG):
                pre(g)
                unit(0, g, True)
            between()
            with eng.Fori(1, NB) as b:
                unit(b, 0, False)
                after(b - 1)
                for g in range(1, NG):
                    unit(b, g, False)
            after(NB - 1)

        def vector_range(link, L):
            H = L["H"]
            link(nc.vector.tensor_scalar(nfc[:, :, 0:2 * H], fc[:, :, 0:2 * H], -1.0, None, ALU.mult))
            nc.vector.tensor_reduce(st[:, 0:2 * H], fc[:, :, 0:2 * H].rearrange("p t c -> p c t"), AX.X, ALU.max)
            link(nc.vector.tensor_reduce(st[:, 2 * H:4 * H], nfc[:, :, 0:2 * H].rearrange("p t c -> p c t"), AX.X, ALU.max))
            nc.vector.sem_inc(L["stat"], 1)
            nc.vector.wait_ge(L["allmax"], 1)
            nc.vector.tensor_tensor(am[:, 0:2 * H], sta[:, 0:2 * H], sta[:, 2 * H:4 * H], ALU.max)
            link(nc.vector.tensor_tensor(ok[:, 0:H], sta[:, H:2 * H], sta[:, 3 * H:4 * H], ALU.add))
            nc.vector.tensor_scalar(ok[:, 0:H], ok[:, 0:H], SPREAD, None, ALU.is_le)
            link(nc.vector.tensor_tensor(ok[:, H:2 * H], am[:, 0:H], am[:, H:2 * H], ALU.add))
            link(nc.vector.tensor_scalar(ok[:, H:2 * H], ok[:, H:2 * H], L["logit"], None, ALU.is_le))
            if L["i"] == 0:
                last = nc.vector.tensor_tensor(flag[:, 0:1], ok[:, 0:1], ok[:, 1:2], ALU.mult)
            else:
                link(nc.vector.tensor_scalar(ok[:, 4:5], sta[:, 8:9], VMAX, None, ALU.is_le))
                link(nc.vector.tensor_tensor(ok[:, 5:7], ok[:, 0:2], ok[:, 2:4], ALU.mult))
                link(nc.vector.tensor_tensor(ok[:, 7:8], ok[:, 5:6], ok[:, 6:7], ALU.mult))
                last = nc.vector.tensor_tensor(flag[:, 1:2], ok[:, 7:8], ok[:, 4:5], ALU.mult)
            last.then_inc(L["flag_ready"], 1)

        def vector_weights(link, L):
            H, a = L["H"], L["slope"]
            link(nc.vector.tensor_scalar(ng[:, 0:H], sta[:, H:2 * H], -1.0, None, ALU.mult))
            nc.vector.tensor_scalar(ng[:, 2:2 + H], sta[:, H:2 * H], -a, None, ALU.mult).then_inc(L["g_max"], 1)
            for hh in range(H):
                last = nc.vector.tensor_scalar(uvt[:, 0, :, hh], fc[:, :, hh], sta[:, H + hh:H + hh + 1], None, ALU.add)
            link(last)
            y, m = uvt[:, 0, :, 0:H], uvt[:, 1, :, 0:H]
            link(nc.vector.scalar_tensor_tensor(out=m, in0=y, scalar=a, in1=y, op0=ALU.mult, op1=ALU.max))
            nc.vector.tensor_tensor(uvt[:, 2, :, 0:H], y, m, ALU.subtract)
            nc.vector.scalar_tensor_tensor(out=uvt[:, 3, :, 0:H], in0=y, scalar=a, in1=m, op0=ALU.mult,
                                           op1=ALU.subtract).then_inc(L["uvp"], 1)
            nc.vector.wait_ge(L["exp_done"], 1)
            nc.vector.tensor_scalar(E[:, :, :, 0:H], E[:, :, :, 0:H], WSC, None, ALU.mult).then_inc(L["e_ready"], 1)
            nc.vector.wait_ge(L["e_ready"], 1)

        def scalar_weights(act, L):
            H, a = L["H"], L["slope"]
            act.wait_ge(L["g_max"], 1)
            for hh in range(H):
                nc.scalar.activation(E[:, 0, :, hh], fc[:, :, H + hh], ACT.Exp, bias=ng[:, hh:hh + 1], scale=1.0)
                last = nc.scalar.activation(E[:, 1, :, hh], fc[:, :, H + hh], ACT.Exp, bias=ng[:, 2 + hh:3 + hh], scale=a)
            last.then_inc(L["exp_done"], 1)
            act.wait_ge(L["uvp"], 1)
            for r in range(2):
                last = nc.scalar.activation(uv[:, :, r, 0:H], uvt[:, 2 + r, :, 0:H], ACT.Exp)
            last.then_inc(L["uv_set"], 1)

        def vector_split(dve, L, g):
            H, Wd = L["H"], L["Wd"]
            CW = H * Wd
            v4 = vals3(L)[:, G * g:G * g + G, :, :]
            for kind in range(2):
                if g >= 1:
                    dve.wait_ge(L["hi_done"], 2 * (g - 1) + kind + 1)
                e4 = E[:, kind, G * g:G * g + G, 0:H].unsqueeze(3).broadcast_to([P, G, H, Wd])
                p4 = prod[:, kind, 0:G * CW].rearrange("p (t h w) -> p t h w", t=G, h=H)
                nc.vector.tensor_tensor(p4, v4, e4, ALU.mult).then_inc(L["x_prod"], 1)
            for kind in range(2):
                dve.wait_ge(L["hi_done"], 2 * g + kind + 1)
                if g >= 1:
                    dve.wait_ge(L["xy_ready"], 2 * (g - 1) + kind + 1)
                p4 = prod[:, kind, 0:G * CW].rearrange("p (t h w) -> p t h w", t=G, h=H)
                d4 = diff[:, kind, 0:G * CW].rearrange("p (t h w) -> p t h w", t=G, h=H)
                nc.vector.tensor_tensor(d4, p4, xy5(L)[:, G * g:G * g + G, kind, :, 0, :],
                                        ALU.subtract).then_inc(L["d_done"], 1)

        def scalar_split(act, L, g):
            H, Wd = L["H"], L["Wd"]
            CW = H * Wd
            for part, ready, done, src, scale in ((0, "x_prod", "hi_done", prod, 1.0), (1, "d_done", "xy_ready", diff, LO)):
                for kind in range(2):
                    act.wait_ge(L[ready], 2 * g + kind + 1)
                    s4 = src[:, kind, 0:G * CW].rearrange("p (t h w) -> p t h w", t=G, h=H)
                    nc.scalar.activation(xy5(L)[:, G * g:G * g + G, kind, :, part, :], s4, ACT.Copy,
                                         scale=scale).then_inc(L[done], 1)

        def pool_stats(pool, L, cols):
            pool.wait_ge(L["stat"], 1)
            nc.gpsimd.partition_all_reduce(sta[:, 0:cols], st[:, 0:cols], P, RMAX).then_inc(L["allmax"], 1)

        def pool_vsum(pool, L):
            pool.wait_ge(L["vpart_done"], 1)
            CW = L["H"] * L["Wd"]
            nc.gpsimd.partition_all_reduce(vsum[:, 0:CW], vpart[:, 0:CW], P, RADD).then_inc(L["vsum_ready"], 1)

        def vector_between(dve, L):
            CW = L["H"] * L["Wd"]
            nc.vector.tensor_reduce(vpart[:, 0:CW], vals[:, :, 0:CW].rearrange("p t c -> p c t"), AX.X,
                                    ALU.add).then_inc(L["vpart_done"], 1)
            dve.wait_ge(L["vsum_ready"], 1)
            dve.wait_ge(L["uv_set"], 1)

        def branch(eng, L, factored, general):
            eng.wait_ge(L["flag_ready"], 1)
            holds = eng.value_load(flag[0:1, L["i"]:L["i"] + 1], min_val=0, max_val=1)
            with eng.If(holds != 0):
                factored()
            with eng.Else():
                general()

        def general_sync(sp, L):
            for r in range(RAW):
                sp.wait_ge(L["adj_in"][r], 16)
            for hh in range(L["H"]):
                with sp.Fori(0, T) as t:
                    sp.wait_ge(L["gen_free"], hh * T + t + 1)
                    sp.dma_start(gadj, adj_d.rearrange("(t p) j -> p t j", p=P)[:, bass.ds(t, 1), :]
                                 .rearrange("p o j -> p (o j)")).then_inc(L["gen_adj_in"], 16)

        def general_vector(dve, L):
            H, Wd = L["H"], L["Wd"]
            w = Wd - 1
            dve.sem_inc(L["gen_free"], 1)
            for hh in range(H):
                with dve.Fori(0, T) as t:
                    n = hh * T + t
                    nc.vector.tensor_scalar(gcol, ones[:, :], fc[:, bass.ds(t, 1), H + hh], None,
                                            ALU.mult).then_inc(L["gen_col"], 1)
                    dve.wait_ge(L["gen_mm"], n + 1)
                    nc.vector.tensor_scalar(gf2[:, bass.ds(t * P, P)], bank[0][:, 0:P], 1.0, None,
                                            ALU.mult).then_inc(L["gen_row"], 1)
                dve.wait_ge(L["gen_row"], hh * T + T)
                with dve.Fori(0, T) as t:
                    n = hh * T + t
                    step = 4 * n
                    dve.wait_ge(L["gen_adj_in"], 16 * n + 16)
                    nc.vector.tensor_scalar(glog, gf2, fc[:, bass.ds(t, 1), hh], None, ALU.add).then_inc(L["gen_step"], 1)
                    dve.wait_ge(L["gen_step"], step + 1)
                    nc.vector.scalar_tensor_tensor(out=glog, in0=glog, scalar=L["slope"], in1=glog, op0=ALU.mult,
                                                   op1=ALU.max).then_inc(L["gen_step"], 1)
                    dve.wait_ge(L["gen_step"], step + 2)
                    if L["i"] == 0:
                        nc.vector.tensor_scalar(gneg, gadj, 0.0, -1e9, ALU.is_le, ALU.mult).then_inc(L["gen_step"], 1)
                    else:
                        nc.vector.scalar_tensor_tensor(out=glog, in0=gadj, scalar=1.0, in1=glog, op0=ALU.is_equal,
                                                       op1=ALU.mult)
                        nc.vector.tensor_scalar(gneg, gadj, 1.0, -9e15, ALU.not_equal, ALU.mult).then_inc(L["gen_step"], 1)
                    dve.wait_ge(L["gen_step"], step + 3)
                    nc.vector.tensor_tensor(glog, glog, gneg, ALU.add).then_inc(L["gen_step"], 1)
                    dve.wait_ge(L["gen_step"], step + 4)
                    nc.vector.tensor_reduce(nmax[:, :], glog, AX.X, ALU.max, negate=True).then_inc(L["gen_logit"], 1)
                    dve.wait_ge(L["gen_exp"], n + 1)
                    nc.vector.reciprocal(rsum[:, 1:2], rsum[:, 0:1]).then_inc(L["gen_rec"], 1)
                    dve.wait_ge(L["gen_rec"], n + 1)
                    dve.wait_ge(L["gen_sum"], n + 1)
                    xs = x[:, bass.ds(t, 1), hh * w:(hh + 1) * w].rearrange("p o w -> p (o w)")
                    nc.vector.scalar_tensor_tensor(out=xs, in0=bank[2][:, 0:w], scalar=rsum[:, 1:2], in1=xs,
                                                   op0=ALU.mult, op1=ALU.add).then_inc(L["gen_free"], 1)
            dve.wait_ge(L["gen_free"], H * T + 1)

        def general_scalar(act, L):
            for hh in range(L["H"]):
                with act.Fori(0, T) as t:
                    n = hh * T + t
                    act.wait_ge(L["gen_logit"], n + 1)
                    nc.scalar.activation(glog, glog, ACT.Exp, bias=nmax[:, 0:1], scale=1.0,
                                         accum_out=rsum[:, 0:1]).then_inc(L["gen_exp"], 1)
                    for c in range(NB):
                        act.wait_ge(L["gen_tr"], NB * n + c + 1)
                        nc.scalar.activation(gT[:, c * IB:(c + 1) * IB], bank[c % 2][:, :],
                                             ACT.Copy).then_inc(L["gen_pt"], 1)

        def general_tensor(pe, L):
            for hh in range(L["H"]):
                with pe.Fori(0, T) as t:
                    pe.wait_ge(L["gen_col"], hh * T + t + 1)
                    nc.tensor.matmul(bank[0][:, 0:P], gcol, ident[:, :], start=True, stop=True).then_inc(L["gen_mm"], 1)
                pe.wait_ge(L["gen_row"], hh * T + T)
                with pe.Fori(0, T) as t:
                    n = hh * T + t
                    pe.wait_ge(L["gen_exp"], n + 1)
                    for c in range(NB):
                        if c >= 2:
                            pe.wait_ge(L["gen_pt"], NB * n + c - 1)
                        for j in range(4):
                            k = 4 * c + j
                            mm = nc.tensor.transpose(bank[c % 2][:, j * P:(j + 1) * P], glog[:, k * P:(k + 1) * P],
                                                     ident[:, :])
                        mm.then_inc(L["gen_tr"], 1)
                    pe.wait_ge(L["gen_pt"], NB * n + NB)
                    for j in range(T):
                        mm = nc.tensor.matmul(bank[2][:, 0:L["Wd"] - 1], gT[:, j * P:(j + 1) * P],
                                              vals3(L)[:, j, hh, 0:L["Wd"] - 1], start=(j == 0), stop=(j == T - 1))
                    mm.then_inc(L["gen_sum"], 1)
            pe.wait_ge(L["gen_free"], L["H"] * T + 1)

        block = ctx.enter_context(nc.Block())
        L0, L1 = LAY

        @block.sync
        def _(sp):
            sp.dma_start(W, W_d).then_inc(consts_in, 16)
            sp.dma_start(w12[:, :], w12_d).then_inc(consts_in, 16)
            sp.dma_start(bcols[:, 0:1], b_d.unsqueeze(1)).then_inc(consts_in, 16)
            sp.dma_start(bcols[:, 1:2], pb1_d.unsqueeze(1)).then_inc(consts_in, 16)
            sp.dma_start(bcols[:, 2:3], pb2_d.unsqueeze(1)).then_inc(consts_in, 16)
            sp.dma_start(b12[:, :], b12_d.partition_broadcast(P)).then_inc(consts_in, 16)
            for c in range(4):
                sp.dma_start(featT[:, c * 1024:(c + 1) * 1024], x2T_d[:, c * 1024:(c + 1) * 1024]).then_inc(feat_in[c], 16)
            for g in range(RAW):
                load_unit(sp, L0, 0, g, True)

            def loads(L):
                for g in range(RAW, NG):
                    load_unit(sp, L, 0, g, False)
                with sp.Fori(1, NB) as b:
                    for g in range(NG):
                        load_unit(sp, L, b, g, False)
                    if L is L1:
                        sp.wait_ge(L1["x_done"], b)
                        sp.dma_start(out_t[:, bass.ds(b * KT - KT, KT), :],
                                     x[:, bass.ds(b * KT - KT, KT), :]).then_inc(out_done, 16)

            def factored0():
                loads(L0)
                for g in range(RAW):
                    sp.wait_ge(L0["q_ready"], NB * NG - RAW + g + 1)
                    load_unit(sp, L1, 0, g, True)

            def general0():
                general_sync(sp, L0)
                for g in range(RAW):
                    load_unit(sp, L1, 0, g, True)

            def factored1():
                loads(L1)
                sp.wait_ge(L1["x_done"], NB)
                sp.dma_start(out_t[:, T - KT:T, :], x[:, T - KT:T, :]).then_inc(out_done, 16)
                sp.wait_ge(out_done, 16 * NB)

            def general1():
                general_sync(sp, L1)
                sp.wait_ge(L1["gen_free"], 2 * T + 1)
                sp.dma_start(out_t[:, :, :], x[:, :, :]).then_inc(out_done, 16)
                sp.wait_ge(out_done, 16)

            branch(sp, L0, factored0, general0)
            branch(sp, L1, factored1, general1)

        @block.gpsimd
        def _(pool):
            nc.gpsimd.memset(ident[:, :], 0.0).then_inc(ident0, 1)
            nc.gpsimd.memset(A[:, :], 0.0).then_inc(ident0, 1)
            pool.wait_ge(ident0, 2)
            nc.gpsimd.affine_select(out=ident[:, :], in_=ident[:, :], compare_op=ALU.not_equal, fill=1.0, base=0,
                                    pattern=[[-1, P]], channel_multiplier=1).then_inc(ident0, 1)
            for hh in range(2):
                for r in range(2):
                    pool.dma_start(A[64 * hh:64 * hh + 64, 2 * r + hh:2 * r + hh + 1],
                                   a_d[hh, 64 * r:64 * r + 64].unsqueeze(1)).then_inc(A_in, 16)
            nc.gpsimd.memset(mhalf[:, :], -0.5).then_inc(ident0, 1)
            pool.wait_ge(ident0, 4)
            pool_stats(pool, L0, 4)
            with pool.Fori(0, NB) as b:
                pool_rstd(pool, L0["ln0"], b)
            branch(pool, L0, lambda: pool_vsum(pool, L0), lambda: None)
            with pool.Fori(0, NB) as b:
                pool_rstd(pool, L0["ln1"], b)
            pool_stats(pool, L1, 9)
            branch(pool, L1, lambda: pool_vsum(pool, L1), lambda: None)

        @block.scalar
        def _(act):
            for c in range(4):
                act.dma_start(x[:, 8 * c:8 * c + 8, :], x_t[:, 8 * c:8 * c + 8, :]).then_inc(x_in[c], 16)
            act.dma_start(W1, W1_d).then_inc(consts_in, 16)
            act.dma_start(W2, W2_d).then_inc(consts_in, 16)
            act.dma_start(rhs1[:, 0:D], W3T_d).then_inc(consts_in, 16)
            act.dma_start(b3[:, :], pb3_d.partition_broadcast(P)).then_inc(consts_in, 16)
            act.wait_ge(pv_ready, 1)
            for c in range(NB):
                act.wait_ge(fbc_mm, c + 1)
                nc.scalar.activation(f1bc0[:, c * IB:(c + 1) * IB], bank[4 + c % 4][:, :], ACT.Identity,
                                     bias=pc[:, 0:1]).then_inc(fbc_ready, 1)
            act.wait_ge(fbc_ready, NB)

            def factored(L):
                scalar_weights(act, L)
                run_core(act, lambda g: scalar_split(act, L, g), lambda b, g, f: scalar_unit(act, L, b, g, f),
                         lambda: None, lambda b: scalar_evac(act, L, b))

            branch(act, L0, lambda: factored(L0), lambda: general_scalar(act, L0))
            for c in range(NB):
                act.wait_ge(trans_mm, c + 1)
                nc.scalar.activation(featT[:, c * IB:(c + 1) * IB], bank[c % 2][:, :], ACT.Copy).then_inc(hT_ready, 1)
                for hh in range(2):
                    act.wait_ge(fbc_mm, NB + 2 * c + hh + 1)
                    nc.scalar.activation(f1bc[hh][:, c * IB:(c + 1) * IB], bank[5 + (2 * c + hh) % 3][:, :], ACT.Identity,
                                         bias=pc[:, 2 + hh:3 + hh]).then_inc(fbc_ready, 1)
            act.wait_ge(fbc_ready, 3 * NB)
            branch(act, L1, lambda: factored(L1), lambda: general_scalar(act, L1))

        @block.vector
        def _(dve):
            count = [0]

            def link(ins):
                count[0] += 1
                ins.then_inc(dve_step, 1)
                dve.wait_ge(dve_step, count[0])

            nc.vector.memset(four[:, 0:1], 4.0)
            nc.vector.memset(four[:, 1:2], -2.0)
            link(nc.vector.memset(ones[:, :], 1.0))
            dve.wait_ge(consts_in, 16 * 10)
            dve.wait_ge(A_in, 64)
            for r in range(3):
                last = nc.vector.tensor_scalar(bb[:, r, :], ones[:, :], bcols[:, r:r + 1], None, ALU.mult)
            last.then_inc(bb_ready, 1)
            dve.wait_ge(pv_mm, 1)
            nc.vector.tensor_copy(pv[:, :], bank[0][:, 0:6])
            link(nc.vector.tensor_copy(pc[:, :], bank[1][:, 0:6]))
            nc.vector.tensor_tensor(pc[:, 0:2], pc[:, 0:2], b12[:, :], ALU.add)
            nc.vector.tensor_copy(rhs1[:, D:D + 4], pv[:, 2:6])
            for r, col in enumerate((0, 2, 3)):
                last = nc.vector.tensor_scalar(pvb[:, r, :], ones[:, :], pv[:, col:col + 1], None, ALU.mult)
            last.then_inc(pv_ready, 1)
            dve.wait_ge(pv_ready, 1)
            dve.wait_ge(fcol_mm, 1)
            f0 = bank[2][:, 0:2 * T].rearrange("p (t c) -> p t c", c=2)
            for c in range(2):
                last = nc.vector.tensor_scalar(fc[:, :, c], f0[:, :, c], pc[:, c:c + 1], None, ALU.add)
            last.then_inc(fc_ready, 1)
            dve.wait_ge(fc_ready, 1)
            nc.vector.memset(vals[:, :, D:D + 1], 1.0)
            vector_range(link, L0)

            def pre0(g):
                if g % 2 == 0:
                    dve.wait_ge(x_in[g // 2], 16)
                layernorm(dve, L0["ln0"], g, lambda b, k, n: vals[:, bass.ds(b * KT + k, n), 0:D])
                dve.wait_ge(L0["ln0"]["h_done"], g + 1)
                vector_split(dve, L0, g)

            def after0(b):
                vector_evac(dve, L0, b)
                dve.wait_ge(L0["x_done"], b + 1)
                nc.vector.memset(pause[:, :], 0.0)
                layernorm(dve, L0["ln1"], b, lambda bb_, k, n: h[:, bass.ds(bb_ * KT + k, n), :])

            def factored0():
                before = count[0]
                vector_weights(link, L0)
                steps.append(count[0] - before)
                run_core(dve, pre0, lambda b, g, f: vector_unit(dve, L0, b, g, f), lambda: vector_between(dve, L0), after0)

            def general0():
                for c in range(4):
                    dve.wait_ge(x_in[c], 16)
                with dve.Fori(0, NB) as b:
                    layernorm(dve, L0["ln0"], b, lambda b, k, n: vals[:, bass.ds(b * KT + k, n), 0:D])
                general_vector(dve, L0)
                dve.sem_inc(dve_step, steps[0])
                with dve.Fori(0, NB) as b:
                    layernorm(dve, L0["ln1"], b, lambda b, k, n: h[:, bass.ds(b * KT + k, n), :])

            steps = []
            branch(dve, L0, factored0, general0)

            v4 = vals3(L1)
            for c in range(NB):
                dve.wait_ge(v_mm, c + 1)
                src = bank[2 + c % 2][:, :].rearrange("p (t h w) -> p t h w", t=KT, h=2)
                bias = b3[:, :].rearrange("p (o h w) -> p o h w", o=1, h=2).broadcast_to([P, KT, 2, D // 2])
                nc.vector.memset(v4[:, KT * c:KT * c + KT, :, D // 2:D // 2 + 1], 1.0)
                nc.vector.tensor_tensor(v4[:, KT * c:KT * c + KT, :, 0:D // 2], src, bias, ALU.add).then_inc(v_ready, 1)
            f1p = bank[4][:, 0:4 * T].rearrange("p (t c) -> p t c", c=4)
            for c in range(4):
                last = nc.vector.tensor_scalar(fc[:, :, c], f1p[:, :, c], pc[:, 2 + c:3 + c], None, ALU.add)
            last.then_inc(fc_ready, 1)
            dve.wait_ge(fc_ready, 2)
            dve.wait_ge(v_ready, NB)
            link(nc.vector.tensor_reduce(st[:, 8:9], vals[:, :, :], AX.XY, ALU.max, apply_absolute_value=True))
            vector_range(link, L1)

            def factored1():
                vector_weights(link, L1)
                run_core(dve, lambda g: vector_split(dve, L1, g), lambda b, g, f: vector_unit(dve, L1, b, g, f),
                         lambda: vector_between(dve, L1), lambda b: vector_evac(dve, L1, b))

            branch(dve, L1, factored1, lambda: general_vector(dve, L1))

        @block.tensor
        def _(pe):
            pe.wait_ge(bb_ready, 1)
            rhs = (w12[:, :], A[:, 0:2], A[:, 2:4])
            for r, w in enumerate((W, W1, W2)):
                nc.tensor.matmul(bank[0][:, 2 * r:2 * r + 2], w, rhs[r], start=True, stop=True)
            for r in range(3):
                mm = nc.tensor.matmul(bank[1][:, 2 * r:2 * r + 2], bb[:, r, :], rhs[r], start=True, stop=True)
            mm.then_inc(pv_mm, 1)
            pe.wait_ge(pv_ready, 1)
            for t in range(T):
                if t % 8 == 0:
                    pe.wait_ge(feat_in[t // 8], 16)
                mm = nc.tensor.matmul(bank[2][:, 2 * t:2 * t + 2], featT[:, t * P:(t + 1) * P], pv[:, 0:2],
                                      start=True, stop=True)
            mm.then_inc(fcol_mm, 1)
            for c in range(NB):
                if c >= 4:
                    pe.wait_ge(fbc_ready, c - 3)
                nc.tensor.matmul(bank[4 + c % 4][:, :], pvb[:, 0, :], featT[:, c * IB:(c + 1) * IB],
                                 start=True, stop=True).then_inc(fbc_mm, 1)
            pe.wait_ge(fbc_ready, NB)
            pe.wait_ge(fc_ready, 1)

            def factored0():
                tensor_core(pe, L0)
                pe.wait_ge(L0["banks_free"], T)

            def general0():
                pe.wait_ge(L0["ln0"]["h_done"], NB)
                general_tensor(pe, L0)

            pe.wait_ge(ident0, 4)
            branch(pe, L0, factored0, general0)
            for c in range(NB):
                pe.wait_ge(L0["ln1"]["h_done"], c + 1)
                if c >= 2:
                    pe.wait_ge(hT_ready, c - 1)
                for j in range(KT):
                    mm = nc.tensor.transpose(bank[c % 2][:, j * P:(j + 1) * P], h[:, KT * c + j, :], ident[:, :])
                mm.then_inc(trans_mm, 1)
                pe.wait_ge(hT_ready, c + 1)
                if c >= 2:
                    pe.wait_ge(v_ready, c - 1)
                for j in range(KT):
                    t = KT * c + j
                    nc.tensor.matmul(bank[4][:, 4 * t:4 * t + 4], featT[:, t * P:(t + 1) * P], rhs1[:, D:D + 4],
                                     start=True, stop=True)
                    mm = nc.tensor.matmul(bank[2 + c % 2][:, j * D:(j + 1) * D], featT[:, t * P:(t + 1) * P], rhs1[:, 0:D],
                                          start=True, stop=True)
                mm.then_inc(v_mm, 1)
                for hh in range(2):
                    m = 2 * c + hh
                    if m >= 3:
                        pe.wait_ge(fbc_ready, NB + m - 2)
                    nc.tensor.matmul(bank[5 + m % 3][:, :], pvb[:, 1 + hh, :], featT[:, c * IB:(c + 1) * IB],
                                     start=True, stop=True).then_inc(fbc_mm, 1)
            pe.wait_ge(fbc_ready, 3 * NB)
            pe.wait_ge(v_ready, NB)
            pe.wait_ge(fc_ready, 2)
            branch(pe, L1, lambda: tensor_core(pe, L1), lambda: general_tensor(pe, L1))


def kernel(x, adj, L0_gnn_inlayer2, L0_gnn_W, L0_gnn_b, L0_gnn_w1, L0_gnn_b1, L0_gnn_w2, L0_gnn_b2,
           L1_gnn_W1, L1_gnn_b1, L1_gnn_W2, L1_gnn_b2, L1_gnn_W3, L1_gnn_b3, L1_gnn_a):
    import numpy as np
    import concourse.bacc as bacc
    from concourse.bass_utils import run_bass_kernel_spmd

    nc = bacc.Bacc("TRN2", target_bir_lowering=False, num_devices=1)
    host = {
        "x": x, "adjT": np.asarray(adj).T, "adj": adj, "inlayer2T": np.asarray(L0_gnn_inlayer2).T,
        "W": L0_gnn_W, "b": L0_gnn_b, "w12": np.stack([np.asarray(L0_gnn_w1), np.asarray(L0_gnn_w2)], axis=1),
        "b12": np.concatenate([np.asarray(L0_gnn_b1), np.asarray(L0_gnn_b2)]),
        "W1": L1_gnn_W1, "W2": L1_gnn_W2, "W3T": np.asarray(L1_gnn_W3).T,
        "pb1": L1_gnn_b1, "pb2": L1_gnn_b2, "pb3": L1_gnn_b3, "a": L1_gnn_a,
    }
    arrays, args = {}, []
    for name, value in host.items():
        value = np.ascontiguousarray(value)
        arrays[f"in_{name}"] = value
        args.append(nc.dram_tensor(f"in_{name}", value.shape, mybir.dt.from_np(value.dtype), kind="ExternalInput").ap())
    args.append(nc.dram_tensor("result", (N, D), F32, kind="ExternalOutput").ap())
    gat_program(nc, *args)
    r = run_bass_kernel_spmd(nc, [arrays], core_ids=[0])
    return r.results[0]["result"]
```

```python
import concourse.bass as bass
from concourse import mybir
from concourse.alu_op_type import AluOpType as ALU
from contextlib import ExitStack

F32 = mybir.dt.float32
F16 = mybir.dt.float16
BF16 = mybir.dt.bfloat16
I32 = mybir.dt.int32
ACT = mybir.ActivationFunctionType
AX = mybir.AxisListType
RMAX = bass.bass_isa.ReduceOp.max
RADD = bass.bass_isa.ReduceOp.add

N = 4096
D = 128
P = 128
T = N // P
IB = 512
NB = N // IB
KT = IB // P
G = 4
NG = T // G
RAW = 4
LO = 2.0 ** 11
WSC = 2.0 ** 11
EPS = 1e-5
SPREAD = 16.0
LOGIT = 30.0
VMAX = 31.0


def gat_program(nc, x_d, adjT_d, adj_d, x2T_d, W_d, b_d, w12_d, b12_d,
                W1_d, W2_d, W3T_d, pb1_d, pb2_d, pb3_d, a_d, out_d):
    ctx = ExitStack()
    with ctx:
        def sb(name, shape, dt=F32):
            return ctx.enter_context(nc.sbuf_tensor(name, shape, dt))

        def sem(name):
            return ctx.enter_context(nc.semaphore(name))

        x = sb("x", [P, T, D])
        featT = sb("featT", [P, N])
        f1bc0 = sb("f1bc0", [P, N])
        f1bc = (f1bc0, featT)
        raw = sb("raw", [P, RAW, G * IB], I32)
        q = sb("q", [P, 2, G * IB], BF16)
        s = sb("s", [P, 2, 2, G * IB], BF16)
        bc = sb("bc", [P, 2, 4, G * IB], BF16)
        vals = sb("vals", [P, T, 130])
        h = vals[:, :, 0:D]
        xy = sb("xy", [P, T, 520], F16)
        tb = sb("tb", [P, KT, 260])
        acc = sb("acc", [P, KT, 260])
        comb = sb("comb", [P, KT, 130])
        fix = sb("fix", [P, KT, 130])
        tb_f, acc_f = (a[:, :, :].rearrange("p (k t) w -> p k (t w)", k=2) for a in (tb, acc))
        prod = [(tb_f[:, 0, :], tb_f[:, 1, :]), (acc_f[:, 0, :], acc_f[:, 1, :]),
                tuple(a[:, :, :].rearrange("p k w -> p (k w)") for a in (comb, fix))]
        vsum = sb("vsum", [P, 130])
        vpart = sb("vpart", [P, 130])
        ones = sb("ones", [P, P])
        ident = sb("ident", [P, P])
        early = bc[:, 0, 0:2, :].rearrange("p h i -> p (h i)").bitcast(F32)
        W, W1, W2 = (early[:, r * D:(r + 1) * D] for r in range(3))
        bb = early[:, 3 * D:6 * D].rearrange("p (r m) -> p r m", r=3)
        bcols = sb("bcols", [P, 3])
        w12 = sb("w12", [P, 2])
        A = sb("A", [P, 4])
        b12 = sb("b12", [P, 2])
        b3 = sb("b3", [P, D])
        pv = sb("pv", [P, 6])
        pc = sb("pc", [P, 6])
        pvb = sb("pvb", [P, 3, P])
        rhs1 = sb("rhs1", [P, D + 4])
        fc = sb("fc", [P, T, 4])
        nfc = sb("nfc", [P, T, 4])
        shift = sb("shift", [P, 2])
        E = sb("E", [P, 2, T, 2])
        uv = sb("uv", [P, T, 2, 2])
        uvt = sb("uvt", [P, 4, T, 2])
        uvcur = sb("uvcur", [P, KT, 2, 2])
        st = sb("st", [P, 10])
        sta = sb("sta", [P, 10])
        ng = sb("ng", [P, 4])
        flagf = sb("flagf", [P, 12])
        nz = sb("nz", [P, KT, 2])
        rden = sb("rden", [P, KT, 2])
        bst = sb("bst", [P, T, 6])
        bag = sb("bag", [P, T, 2])
        vare = sb("vare", [P, T])
        pause = sb("pause", [P, 1])
        flag = sb("flag", [P, 2], I32)
        am = sb("am", [P, 4])
        ok = sb("ok", [P, 8])
        nmax = sb("nmax", [P, 1])
        rsum = sb("rsum", [P, 2])
        gadj = bc[:, 0, :, :].rearrange("p k i -> p (k i)").bitcast(I32)[:, 0:N]
        gneg = bc[:, 0, :, :].rearrange("p k i -> p (k i)").bitcast(F32)[:, 0:N]
        glog = bc[:, 1, :, :].rearrange("p k i -> p (k i)").bitcast(F32)[:, 0:N]
        gT = s[:, :, :, :].rearrange("p k h i -> p (k h i)").bitcast(F32)[:, 0:N]
        gf2 = xy[:, :, :].rearrange("p t w -> p (t w)").bitcast(F32)[:, 0:N]
        gcol = fix[:, :, :].rearrange("p k w -> p (k w)")[:, 0:P]
        mhalf = sb("mhalf", [P, T])
        rstd = sb("rstd", [P, T])

        bank = [ctx.enter_context(nc.psum_tensor(f"bank{i}", [P, 512], F32)) for i in range(8)]

        LAY = [dict(i=0, H=1, Wd=129, slope=0.01, logit=LOGIT, sign=1.0), dict(i=1, H=2, Wd=65, slope=0.2, logit=1e30, sign=-1.0)]
        for L in LAY:
            i = L["i"]
            L["adj_in"] = [sem(f"adj_in{i}_{r}") for r in range(RAW)]
            for name in ("q_ready", "s_ready", "t_ready", "g_ready", "bc_ready", "bc_used", "tiles_done",
                         "uv_ready", "b_scaled", "banks_free", "comb_done", "nz_done", "fix_done", "sum_done",
                         "rden_done", "x_done", "stat", "allmax", "g_max", "exp_done", "uvp", "uv_exp", "uv_set", "e_ready",
                         "flag_ready", "gen_adj_in", "gen_col", "gen_mm", "gen_row", "gen_logit", "gen_exp", "gen_tr",
                         "gen_pt", "gen_sum", "gen_rec", "gen_free", "gen_step",
                         "x_prod", "hi_done", "d_done", "xy_ready", "vpart_done", "vsum_ready"):
                L[name] = sem(f"{name}{i}")
        for ln in ("ln0", "ln1"):
            LAY[0][ln] = {name: sem(f"{ln}_{name}") for name in ("bst_done", "bag_done", "var_done", "rstd_done", "norm_done", "h_done")}
        x_in = [sem(f"x_in{c}") for c in range(4)]
        feat_in = [sem(f"feat_in{c}") for c in range(4)]
        consts_in = sem("consts_in")
        A_in = sem("A_in")
        ident0 = sem("ident0")
        bb_ready = sem("bb_ready")
        pv_mm = sem("pv_mm")
        pv_ready = sem("pv_ready")
        fcol_mm = sem("fcol_mm")
        fbc_mm = sem("fbc_mm")
        fbc_ready = sem("fbc_ready")
        fc_ready = sem("fc_ready")
        trans_mm = sem("trans_mm")
        hT_ready = sem("hT_ready")
        v_mm = sem("v_mm")
        v_ready = sem("v_ready")
        dve_step = sem("dve_step")
        out_done = sem("out_done")

        x_t = x_d.rearrange("(t p) d -> p t d", p=P)
        out_t = out_d.rearrange("(t p) d -> p t d", p=P)
        adjT_t = adjT_d.rearrange("(t p) i -> p t i", p=P)

        def xy5(L):
            if L["i"] == 0:
                return xy[:, :, 0:4 * L["Wd"]].rearrange("p t (k h r w) -> p t k h r w", k=2, h=1, r=2)
            return xy[:, :, :].rearrange("p t (h k r w) -> p t k h r w", k=2, h=2, r=2)

        def vals3(L):
            return vals[:, :, 0:L["H"] * L["Wd"]].rearrange("p t (h w) -> p t h w", h=L["H"])

        def load_unit(sp, L, b, g, first):
            if not first:
                sp.wait_ge(L["q_ready"], NG * b + g - RAW + 1)
            sp.dma_start(raw[:, g % RAW, :].rearrange("p (t i) -> p t i", t=G),
                         adjT_t[:, G * g:G * g + G, bass.ds(b * IB, IB)]).then_inc(L["adj_in"][g % RAW], 16)

        def act_jts(L, g):
            if L["i"] == 0:
                return [(j, 0) for j in range(2 if g % 3 == 2 else 3)]
            return [(j, hh) for hh in range(2) for j in range(4) if not (hh == 1 and j >= 1)]

        def dve_jts(L, g):
            return [(j, hh) for hh in range(L["H"]) for j in range(G) if (j, hh) not in act_jts(L, g)]

        def scalar_unit(act, L, b, g, first=False):
            evac = g == 1 and not first
            n = NG * b + g
            if g >= 2 or not first:
                act.wait_ge(L["bc_ready"], n - 1)
            act.wait_ge(L["adj_in"][g % RAW], 16 * (2 * b + g // RAW + 1))
            if L["i"] == 0:
                nc.scalar.activation(q[:, g % 2, :], raw[:, g % RAW, :], ACT.Relu, bias=shift[:, 0:1],
                                     scale=-4.0).then_inc(L["q_ready"], 1)
            else:
                nc.scalar.activation(q[:, g % 2, :], raw[:, g % RAW, :], ACT.Square, bias=shift[:, 1:2],
                                     scale=2.0).then_inc(L["q_ready"], 1)
            signs = act_jts(L, g)
            for m in range(max(len(signs), KT)):
                if evac and m < KT:
                    scalar_evac(act, L, b - 1, m)
                for j, hh in signs[m:m + 1]:
                    src = nfc if L["i"] == 0 else fc
                    last = nc.scalar.activation(s[:, g % 2, hh, j * IB:(j + 1) * IB], f1bc[hh][:, bass.ds(b * IB, IB)],
                                                ACT.Sign, bias=src[:, G * g + j, L["H"] + hh:L["H"] + hh + 1],
                                                scale=-1.0 if L["i"] == 0 else 1.0)
                if m == len(signs) - 1:
                    last.then_inc(L["s_ready"], 1)

        def bc_free(dve, L, b, g, first):
            if g >= 2:
                dve.wait_ge(L["bc_used"], (NG - 1) * b + g - 1)
            elif g == 1 and not first:
                dve.wait_ge(L["tiles_done"], KT * b)
            elif not first:
                dve.wait_ge(L["bc_used"], (NG - 1) * b)

        def vector_unit(dve, L, b, g, first=False):
            n = NG * b + g
            for j, hh in dve_jts(L, g):
                dst, f1 = s[:, g % 2, hh, j * IB:(j + 1) * IB], f1bc[hh][:, bass.ds(b * IB, IB)]
                nf2 = nfc[:, G * g + j, L["H"] + hh:L["H"] + hh + 1]
                if L["i"] == 0:
                    last = nc.vector.tensor_scalar(dst, f1, nf2, None, ALU.is_lt)
                else:
                    last = nc.vector.tensor_scalar(dst, f1, nf2, -1.0, ALU.is_ge, ALU.add)
            last.then_inc(L["t_ready"], 1)
            dve.wait_ge(L["q_ready"], n + 1)
            if L["i"] == 0:
                dve.wait_ge(L["s_ready"], n + 1)
                dve.wait_ge(L["t_ready"], n + 1)
                nc.vector.tensor_tensor(s[:, g % 2, 0, :], s[:, g % 2, 0, :], q[:, g % 2, :], ALU.add).then_inc(L["g_ready"], 1)
                dve.wait_ge(L["g_ready"], n + 1)
                bc_free(dve, L, b, g, first)
                nc.vector.tensor_scalar(bc[:, g % 2, 0, :], s[:, g % 2, 0, :], 0.0, None, ALU.is_le)
                nc.vector.tensor_scalar(bc[:, g % 2, 1, :], s[:, g % 2, 0, :], 1.0, None,
                                        ALU.is_equal).then_inc(L["bc_ready"], 1)
            else:
                bc_free(dve, L, b, g, first)
                nc.vector.tensor_scalar(bc[:, g % 2, 2, :], q[:, g % 2, :], 0.0, -1.0, ALU.is_equal, ALU.mult)
                dve.wait_ge(L["s_ready"], n + 1)
                dve.wait_ge(L["t_ready"], n + 1)
                nc.vector.tensor_tensor(bc[:, g % 2, 0, :], q[:, g % 2, :], s[:, g % 2, 0, :], ALU.is_le)
                nc.vector.tensor_tensor(bc[:, g % 2, 1, :], q[:, g % 2, :], s[:, g % 2, 1, :],
                                        ALU.is_le).then_inc(L["bc_ready"], 1)

        def tensor_unit(pe, L, b, g, first):
            H, Wd = L["H"], L["Wd"]
            v = xy5(L)
            if first:
                pe.wait_ge(L["xy_ready"], 2 * (g + 1))
            pe.wait_ge(L["bc_ready"], NG * b + g + 1)
            for k in range(KT):
                if g == 0 and not first:
                    pe.wait_ge(L["banks_free"], KT * b - KT + k + 1)
                for j in range(G):
                    t, begin, end = G * g + j, g == 0 and j == 0, g == NG - 1 and j == G - 1
                    c = slice(j * IB + k * P, j * IB + (k + 1) * P)
                    if L["i"] == 0:
                        for kind in range(2):
                            mm = nc.tensor.matmul(bank[2 * k + kind][:, 0:2 * Wd], bc[:, g % 2, kind, c], v[:, t, kind, 0, :, :],
                                                  start=begin, stop=end)
                    else:
                        for hh in range(2):
                            nc.tensor.matmul(bank[2 * k + hh][:, 0:4 * Wd], bc[:, g % 2, hh, c],
                                             xy[:, t, hh * 4 * Wd:(hh + 1) * 4 * Wd], start=begin, stop=end,
                                             skip_group_check=True)
                            mm = nc.tensor.matmul(bank[2 * k + hh][:, 2 * Wd:4 * Wd], bc[:, g % 2, 2, c],
                                                  v[:, t, 1, hh, :, :], start=False, stop=end, skip_group_check=True)
                if g == NG - 1:
                    mm.then_inc(L["tiles_done"], 1)
            if g < NG - 1:
                mm.then_inc(L["bc_used"], 1)

        def tensor_core(pe, L):
            for g in range(NG):
                tensor_unit(pe, L, 0, g, True)
            with pe.Fori(1, NB) as b:
                for g in range(NG):
                    tensor_unit(pe, L, b, g, False)

        def sums(L, k, hh):
            Wd = L["Wd"]
            if L["i"] == 0:
                return bank[2 * k][:, 0:2 * Wd], bank[2 * k + 1][:, 0:2 * Wd]
            return bank[2 * k + hh][:, 0:2 * Wd], bank[2 * k + hh][:, 2 * Wd:4 * Wd]

        def scalar_evac(act, L, b, k):
            H, Wd = L["H"], L["Wd"]
            if k == 0:
                act.wait_ge(L["uv_ready"], b + 1)
            act.wait_ge(L["tiles_done"], KT * b + k + 1)
            for hh in range(H):
                last = nc.scalar.activation(tb[:, k, hh * 2 * Wd:(hh + 1) * 2 * Wd], sums(L, k, hh)[0], ACT.Copy,
                                            scale=uvcur[:, k, 0, hh:hh + 1])
            last.then_inc(L["b_scaled"], 1)

        def vector_evac(dve, L, b):
            H, Wd = L["H"], L["Wd"]
            nc.vector.tensor_scalar(uvcur[:, :, :, 0:H], uv[:, bass.ds(b * KT, KT), :, 0:H], 1.0, None,
                                    ALU.mult).then_inc(L["uv_ready"], 1)
            dve.wait_ge(L["uv_ready"], b + 1)
            for k in range(KT):
                dve.wait_ge(L["b_scaled"], KT * b + k + 1)
                for hh in range(H):
                    c = slice(hh * 2 * Wd, (hh + 1) * 2 * Wd)
                    last = nc.vector.scalar_tensor_tensor(out=acc[:, k, c], in0=sums(L, k, hh)[1],
                                                          scalar=uvcur[:, k, 1, hh:hh + 1], in1=tb[:, k, c],
                                                          op0=ALU.mult, op1=ALU.add)
                last.then_inc(L["banks_free"], 1)

        def vector_combine(dve, L, b):
            H, Wd = L["H"], L["Wd"]
            CW = H * Wd
            dve.wait_ge(L["banks_free"], KT * b + KT)
            a4 = acc[:, :, 0:2 * CW].rearrange("p k (h r w) -> p (k h) r w", h=H, r=2)
            c3 = comb[:, :, 0:CW].rearrange("p k (h w) -> p (k h) w", h=H)
            nc.vector.scalar_tensor_tensor(out=c3, in0=a4[:, :, 1, :], scalar=1.0 / LO, in1=a4[:, :, 0, :],
                                           op0=ALU.mult, op1=ALU.add).then_inc(L["comb_done"], 1)
            dve.wait_ge(L["comb_done"], b + 1)
            c4 = comb[:, :, 0:CW].rearrange("p k (h w) -> p k h w", h=H)
            f4 = fix[:, :, 0:CW].rearrange("p k (h w) -> p k h w", h=H)
            nc.vector.tensor_scalar(nz[:, :, 0:H], c4[:, :, :, Wd - 1], 0.0, None, ALU.is_equal).then_inc(L["nz_done"], 1)
            dve.wait_ge(L["nz_done"], b + 1)
            dve.wait_ge(L["vsum_ready"], 1)
            vs = vsum[:, 0:CW].rearrange("p (o h w) -> p o h w", o=1, h=H).broadcast_to([P, KT, H, Wd])
            nc.vector.tensor_tensor(f4, vs, nz[:, :, 0:H].unsqueeze(3).broadcast_to([P, KT, H, Wd]),
                                    ALU.mult).then_inc(L["fix_done"], 1)

        def vector_result(dve, L, b):
            H, Wd = L["H"], L["Wd"]
            CW = H * Wd
            f4 = fix[:, :, 0:CW].rearrange("p k (h w) -> p k h w", h=H)
            dve.wait_ge(L["fix_done"], b + 1)
            nc.vector.tensor_tensor(fix[:, :, 0:CW], comb[:, :, 0:CW], fix[:, :, 0:CW], ALU.add).then_inc(L["sum_done"], 1)
            dve.wait_ge(L["sum_done"], b + 1)
            nc.vector.reciprocal(rden[:, :, 0:H], f4[:, :, :, Wd - 1]).then_inc(L["rden_done"], 1)
            dve.wait_ge(L["rden_done"], b + 1)
            for k in range(KT):
                for hh in range(H):
                    w = Wd - 1
                    xs = x[:, bass.ds(b * KT + k, 1), hh * w:(hh + 1) * w].rearrange("p o w -> p (o w)")
                    last = nc.vector.scalar_tensor_tensor(out=xs, in0=f4[:, k, hh, 0:w], scalar=rden[:, k, hh:hh + 1],
                                                          in1=xs, op0=ALU.mult, op1=ALU.add)
            last.then_inc(L["x_done"], 1)

        def ln_stats(dve, L, b, tiles, step, at=0):
            for k in range(tiles):
                last = nc.vector.bn_stats(bst[:, at + k, :], x[:, bass.ds(b * tiles + k, 1), :].rearrange("p o w -> p (o w)"))
            last.then_inc(L["bst_done"], 1)
            dve.wait_ge(L["bst_done"], step)
            nc.vector.memset(pause[:, :], 0.0)
            for k in range(tiles):
                last = nc.vector.bn_aggr(bag[:, at + k, :], bst[:, at + k, :])
            last.then_inc(L["bag_done"], 1)
            dve.wait_ge(L["bag_done"], step)
            nc.vector.tensor_scalar(vare[:, at:at + tiles], bag[:, at:at + tiles, 1], EPS, None, ALU.add).then_inc(L["var_done"], 1)

        def ln_apply(dve, L, b, tiles, step, dst, at=0):
            dve.wait_ge(L["rstd_done"], step)
            for k in range(tiles):
                last = nc.vector.tensor_scalar(dst(b * tiles + k, 1), x[:, bass.ds(b * tiles + k, 1), :],
                                               bag[:, at + k, 0:1], rstd[:, at + k:at + k + 1], ALU.subtract, ALU.mult)
            last.then_inc(L["norm_done"], 1)
            dve.wait_ge(L["norm_done"], step)
            nc.vector.tensor_scalar(dst(b * tiles, tiles), dst(b * tiles, tiles), 0.0, None, ALU.max).then_inc(L["h_done"], 1)

        def pool_rstd(pool, L, tiles, step, at=0):
            pool.wait_ge(L["var_done"], step)
            nc.gpsimd.tensor_tensor(rstd[:, at:at + tiles], vare[:, at:at + tiles], mhalf[:, at:at + tiles], ALU.pow).then_inc(L["rstd_done"], 1)

        def run_core(eng, unit, after):
            for g in range(NG):
                unit(0, g, True)
            with eng.Fori(1, NB) as b:
                for g in range(NG):
                    unit(b, g, False)
                    if g < len(after):
                        after[g](b - 1)
            for step in after:
                step(NB - 1)

        def vector_range(link, L):
            H = L["H"]
            link(nc.vector.tensor_scalar(nfc[:, :, 0:2 * H], fc[:, :, 0:2 * H], -1.0, None, ALU.mult))
            nc.vector.tensor_reduce(st[:, 0:2 * H], fc[:, :, 0:2 * H].rearrange("p t c -> p c t"), AX.X, ALU.max)
            link(nc.vector.tensor_reduce(st[:, 2 * H:4 * H], nfc[:, :, 0:2 * H].rearrange("p t c -> p c t"), AX.X, ALU.max))
            nc.vector.sem_inc(L["stat"], 1)
            nc.vector.wait_ge(L["allmax"], 1)
            nc.vector.tensor_tensor(am[:, 0:2 * H], sta[:, 0:2 * H], sta[:, 2 * H:4 * H], ALU.max)
            link(nc.vector.tensor_tensor(ok[:, 0:H], sta[:, H:2 * H], sta[:, 3 * H:4 * H], ALU.add))
            nc.vector.tensor_scalar(ok[:, 0:H], ok[:, 0:H], SPREAD, None, ALU.is_le)
            link(nc.vector.tensor_tensor(ok[:, H:2 * H], am[:, 0:H], am[:, H:2 * H], ALU.add))
            link(nc.vector.tensor_scalar(ok[:, H:2 * H], ok[:, H:2 * H], L["logit"], None, ALU.is_le))
            if L["i"] == 0:
                last = nc.vector.tensor_tensor(flag[:, 0:1], ok[:, 0:1], ok[:, 1:2], ALU.mult)
            else:
                link(nc.vector.tensor_scalar(ok[:, 4:5], sta[:, 8:9], VMAX, None, ALU.is_le))
                link(nc.vector.tensor_tensor(ok[:, 5:7], ok[:, 0:2], ok[:, 2:4], ALU.mult))
                link(nc.vector.tensor_tensor(ok[:, 7:8], ok[:, 5:6], ok[:, 6:7], ALU.mult))
                last = nc.vector.tensor_tensor(flag[:, 1:2], ok[:, 7:8], ok[:, 4:5], ALU.mult)
            last.then_inc(L["flag_ready"], 1)

        def vector_weights(link, L):
            H, a = L["H"], L["slope"]
            link(nc.vector.tensor_scalar(ng[:, 0:H], sta[:, H:2 * H], -1.0, None, ALU.mult))
            nc.vector.tensor_scalar(ng[:, 2:2 + H], sta[:, H:2 * H], -a, None, ALU.mult).then_inc(L["g_max"], 1)
            for hh in range(H):
                last = nc.vector.tensor_scalar(uvt[:, 0, :, hh], fc[:, :, hh], sta[:, H + hh:H + hh + 1], None, ALU.add)
            link(last)
            y, m = uvt[:, 0, :, 0:H], uvt[:, 1, :, 0:H]
            link(nc.vector.scalar_tensor_tensor(out=m, in0=y, scalar=a, in1=y, op0=ALU.mult, op1=ALU.max))
            nc.vector.tensor_tensor(uvt[:, 2, :, 0:H], y, m, ALU.subtract)
            nc.vector.scalar_tensor_tensor(out=uvt[:, 3, :, 0:H], in0=y, scalar=a, in1=m, op0=ALU.mult,
                                           op1=ALU.subtract).then_inc(L["uvp"], 1)
            nc.vector.wait_ge(L["uv_exp"], 1)
            nc.vector.tensor_scalar(uv[:, :, 1, 0:H], uv[:, :, 1, 0:H], L["sign"], None, ALU.mult).then_inc(L["uv_set"], 1)
            nc.vector.tensor_scalar(E[:, :, :, 0:H], E[:, :, :, 0:H], WSC, None, ALU.mult).then_inc(L["e_ready"], 1)
            nc.vector.wait_ge(L["e_ready"], 1)

        def scalar_weights(act, L):
            H, a = L["H"], L["slope"]
            act.wait_ge(L["g_max"], 1)
            for hh in range(H):
                nc.scalar.activation(E[:, 0, :, hh], fc[:, :, H + hh], ACT.Exp, bias=ng[:, hh:hh + 1], scale=1.0)
                last = nc.scalar.activation(E[:, 1, :, hh], fc[:, :, H + hh], ACT.Exp, bias=ng[:, 2 + hh:3 + hh], scale=a)
            last.then_inc(L["exp_done"], 1)
            act.wait_ge(L["uvp"], 1)
            for r in range(2):
                last = nc.scalar.activation(uv[:, :, r, 0:H], uvt[:, 2 + r, :, 0:H], ACT.Exp)
            last.then_inc(L["uv_exp"], 1)

        def split_view(L, g, kind):
            return prod[g % 3][kind][:, 0:G * L["H"] * L["Wd"]].rearrange("p (t h w) -> p t h w", t=G, h=L["H"])

        def vector_split(dve, L):
            H, Wd = L["H"], L["Wd"]
            for g in range(NG + 1):
                if g < NG:
                    if g >= 3:
                        dve.wait_ge(L["xy_ready"], 2 * (g - 2))
                    for kind in range(2):
                        e4 = E[:, kind, G * g:G * g + G, 0:H].unsqueeze(3).broadcast_to([P, G, H, Wd])
                        nc.vector.tensor_tensor(split_view(L, g, kind), vals3(L)[:, G * g:G * g + G, :, :], e4,
                                                ALU.mult).then_inc(L["x_prod"], 1)
                if g >= 1:
                    for kind in range(2):
                        dve.wait_ge(L["hi_done"], 2 * (g - 1) + kind + 1)
                        p4 = split_view(L, g - 1, kind)
                        nc.vector.tensor_tensor(p4, p4, xy5(L)[:, G * (g - 1):G * g, kind, :, 0, :],
                                                ALU.subtract).then_inc(L["d_done"], 1)
            nc.vector.tensor_reduce(vpart[:, 0:H * Wd], vals[:, :, 0:H * Wd].rearrange("p t c -> p c t"), AX.X,
                                    ALU.add).then_inc(L["vpart_done"], 1)

        def scalar_split(act, L):
            for g in range(NG + 1):
                if g < NG:
                    for kind in range(2):
                        act.wait_ge(L["x_prod"], 2 * g + kind + 1)
                        nc.scalar.activation(xy5(L)[:, G * g:G * g + G, kind, :, 0, :], split_view(L, g, kind),
                                             ACT.Copy).then_inc(L["hi_done"], 1)
                if g >= 1:
                    for kind in range(2):
                        act.wait_ge(L["d_done"], 2 * (g - 1) + kind + 1)
                        nc.scalar.activation(xy5(L)[:, G * (g - 1):G * g, kind, :, 1, :], split_view(L, g - 1, kind),
                                             ACT.Copy, scale=LO).then_inc(L["xy_ready"], 1)

        def pool_stats(pool, L, cols):
            pool.wait_ge(L["stat"], 1)
            nc.gpsimd.partition_all_reduce(sta[:, 0:cols], st[:, 0:cols], P, RMAX).then_inc(L["allmax"], 1)

        def pool_vsum(pool, L):
            pool.wait_ge(L["vpart_done"], 1)
            CW = L["H"] * L["Wd"]
            nc.gpsimd.partition_all_reduce(vsum[:, 0:CW], vpart[:, 0:CW], P, RADD).then_inc(L["vsum_ready"], 1)

        def branch(eng, L, factored, general):
            eng.wait_ge(L["flag_ready"], 1)
            holds = eng.value_load(flag[0:1, L["i"]:L["i"] + 1], min_val=0, max_val=1)
            with eng.If(holds != 0):
                factored()
            with eng.Else():
                general()

        def general_sync(sp, L):
            for r in range(RAW):
                sp.wait_ge(L["adj_in"][r], 16)
            for hh in range(L["H"]):
                with sp.Fori(0, T) as t:
                    sp.wait_ge(L["gen_free"], hh * T + t + 1)
                    sp.dma_start(gadj, adj_d.rearrange("(t p) j -> p t j", p=P)[:, bass.ds(t, 1), :]
                                 .rearrange("p o j -> p (o j)")).then_inc(L["gen_adj_in"], 16)

        def general_vector(dve, L):
            H, Wd = L["H"], L["Wd"]
            w = Wd - 1
            dve.sem_inc(L["gen_free"], 1)
            for hh in range(H):
                with dve.Fori(0, T) as t:
                    n = hh * T + t
                    nc.vector.tensor_scalar(gcol, ones[:, :], fc[:, bass.ds(t, 1), H + hh], None,
                                            ALU.mult).then_inc(L["gen_col"], 1)
                    dve.wait_ge(L["gen_mm"], n + 1)
                    nc.vector.tensor_scalar(gf2[:, bass.ds(t * P, P)], bank[0][:, 0:P], 1.0, None,
                                            ALU.mult).then_inc(L["gen_row"], 1)
                dve.wait_ge(L["gen_row"], hh * T + T)
                with dve.Fori(0, T) as t:
                    n = hh * T + t
                    step = 4 * n
                    dve.wait_ge(L["gen_adj_in"], 16 * n + 16)
                    nc.vector.tensor_scalar(glog, gf2, fc[:, bass.ds(t, 1), hh], None, ALU.add).then_inc(L["gen_step"], 1)
                    dve.wait_ge(L["gen_step"], step + 1)
                    nc.vector.scalar_tensor_tensor(out=glog, in0=glog, scalar=L["slope"], in1=glog, op0=ALU.mult,
                                                   op1=ALU.max).then_inc(L["gen_step"], 1)
                    dve.wait_ge(L["gen_step"], step + 2)
                    if L["i"] == 0:
                        nc.vector.tensor_scalar(gneg, gadj, 0.0, -1e9, ALU.is_le, ALU.mult).then_inc(L["gen_step"], 1)
                    else:
                        nc.vector.scalar_tensor_tensor(out=glog, in0=gadj, scalar=1.0, in1=glog, op0=ALU.is_equal,
                                                       op1=ALU.mult)
                        nc.vector.tensor_scalar(gneg, gadj, 1.0, -9e15, ALU.not_equal, ALU.mult).then_inc(L["gen_step"], 1)
                    dve.wait_ge(L["gen_step"], step + 3)
                    nc.vector.tensor_tensor(glog, glog, gneg, ALU.add).then_inc(L["gen_step"], 1)
                    dve.wait_ge(L["gen_step"], step + 4)
                    nc.vector.tensor_reduce(nmax[:, :], glog, AX.X, ALU.max, negate=True).then_inc(L["gen_logit"], 1)
                    dve.wait_ge(L["gen_exp"], n + 1)
                    nc.vector.reciprocal(rsum[:, 1:2], rsum[:, 0:1]).then_inc(L["gen_rec"], 1)
                    dve.wait_ge(L["gen_rec"], n + 1)
                    dve.wait_ge(L["gen_sum"], n + 1)
                    xs = x[:, bass.ds(t, 1), hh * w:(hh + 1) * w].rearrange("p o w -> p (o w)")
                    nc.vector.scalar_tensor_tensor(out=xs, in0=bank[2][:, 0:w], scalar=rsum[:, 1:2], in1=xs,
                                                   op0=ALU.mult, op1=ALU.add).then_inc(L["gen_free"], 1)
            dve.wait_ge(L["gen_free"], H * T + 1)

        def general_scalar(act, L):
            for hh in range(L["H"]):
                with act.Fori(0, T) as t:
                    n = hh * T + t
                    act.wait_ge(L["gen_logit"], n + 1)
                    nc.scalar.activation(glog, glog, ACT.Exp, bias=nmax[:, 0:1], scale=1.0,
                                         accum_out=rsum[:, 0:1]).then_inc(L["gen_exp"], 1)
                    for c in range(NB):
                        act.wait_ge(L["gen_tr"], NB * n + c + 1)
                        nc.scalar.activation(gT[:, c * IB:(c + 1) * IB], bank[c % 2][:, :],
                                             ACT.Copy).then_inc(L["gen_pt"], 1)

        def general_tensor(pe, L):
            for hh in range(L["H"]):
                with pe.Fori(0, T) as t:
                    pe.wait_ge(L["gen_col"], hh * T + t + 1)
                    nc.tensor.matmul(bank[0][:, 0:P], gcol, ident[:, :], start=True, stop=True).then_inc(L["gen_mm"], 1)
                pe.wait_ge(L["gen_row"], hh * T + T)
                with pe.Fori(0, T) as t:
                    n = hh * T + t
                    pe.wait_ge(L["gen_exp"], n + 1)
                    for c in range(NB):
                        if c >= 2:
                            pe.wait_ge(L["gen_pt"], NB * n + c - 1)
                        for j in range(4):
                            k = 4 * c + j
                            mm = nc.tensor.transpose(bank[c % 2][:, j * P:(j + 1) * P], glog[:, k * P:(k + 1) * P],
                                                     ident[:, :])
                        mm.then_inc(L["gen_tr"], 1)
                    pe.wait_ge(L["gen_pt"], NB * n + NB)
                    for j in range(T):
                        mm = nc.tensor.matmul(bank[2][:, 0:L["Wd"] - 1], gT[:, j * P:(j + 1) * P],
                                              vals3(L)[:, j, hh, 0:L["Wd"] - 1], start=(j == 0), stop=(j == T - 1))
                    mm.then_inc(L["gen_sum"], 1)
            pe.wait_ge(L["gen_free"], L["H"] * T + 1)

        block = ctx.enter_context(nc.Block())
        L0, L1 = LAY

        @block.sync
        def _(sp):
            sp.dma_start(W, W_d).then_inc(consts_in, 16)
            sp.dma_start(w12[:, :], w12_d).then_inc(consts_in, 16)
            sp.dma_start(bcols[:, 0:1], b_d.unsqueeze(1)).then_inc(consts_in, 16)
            sp.dma_start(bcols[:, 1:2], pb1_d.unsqueeze(1)).then_inc(consts_in, 16)
            sp.dma_start(bcols[:, 2:3], pb2_d.unsqueeze(1)).then_inc(consts_in, 16)
            sp.dma_start(b12[:, :], b12_d.partition_broadcast(P)).then_inc(consts_in, 16)
            for c in range(4):
                sp.dma_start(featT[:, c * 1024:(c + 1) * 1024], x2T_d[:, c * 1024:(c + 1) * 1024]).then_inc(feat_in[c], 16)
            for g in range(RAW):
                load_unit(sp, L0, 0, g, True)

            def loads(L):
                for g in range(RAW, NG):
                    load_unit(sp, L, 0, g, False)
                with sp.Fori(1, NB) as b:
                    for g in range(NG):
                        load_unit(sp, L, b, g, False)
                    if L is L1:
                        sp.wait_ge(L1["x_done"], b)
                        sp.dma_start(out_t[:, bass.ds(b * KT - KT, KT), :],
                                     x[:, bass.ds(b * KT - KT, KT), :]).then_inc(out_done, 16)

            def factored0():
                loads(L0)
                for g in range(RAW):
                    sp.wait_ge(L0["q_ready"], NB * NG - RAW + g + 1)
                    load_unit(sp, L1, 0, g, True)

            def general0():
                general_sync(sp, L0)
                for g in range(RAW):
                    load_unit(sp, L1, 0, g, True)

            def factored1():
                loads(L1)
                sp.wait_ge(L1["x_done"], NB)
                sp.dma_start(out_t[:, T - KT:T, :], x[:, T - KT:T, :]).then_inc(out_done, 16)
                sp.wait_ge(out_done, 16 * NB)

            def general1():
                general_sync(sp, L1)
                sp.wait_ge(L1["gen_free"], 2 * T + 1)
                sp.dma_start(out_t[:, :, :], x[:, :, :]).then_inc(out_done, 16)
                sp.wait_ge(out_done, 16)

            branch(sp, L0, factored0, general0)
            branch(sp, L1, factored1, general1)

        @block.gpsimd
        def _(pool):
            nc.gpsimd.memset(ident[:, :], 0.0).then_inc(ident0, 1)
            nc.gpsimd.memset(A[:, :], 0.0).then_inc(ident0, 1)
            pool.wait_ge(ident0, 2)
            nc.gpsimd.affine_select(out=ident[:, :], in_=ident[:, :], compare_op=ALU.not_equal, fill=1.0, base=0,
                                    pattern=[[-1, P]], channel_multiplier=1).then_inc(ident0, 1)
            for hh in range(2):
                for r in range(2):
                    pool.dma_start(A[64 * hh:64 * hh + 64, 2 * r + hh:2 * r + hh + 1],
                                   a_d[hh, 64 * r:64 * r + 64].unsqueeze(1)).then_inc(A_in, 16)
            nc.gpsimd.memset(mhalf[:, :], -0.5).then_inc(ident0, 1)
            pool.wait_ge(ident0, 4)
            for c in range(4):
                pool_rstd(pool, L0["ln0"], T // 4, c + 1, at=c * T // 4)
            pool_stats(pool, L0, 4)
            branch(pool, L0, lambda: pool_vsum(pool, L0), lambda: None)
            with pool.Fori(0, NB) as b:
                pool_rstd(pool, L0["ln1"], KT, b + 1)
            pool_stats(pool, L1, 9)
            branch(pool, L1, lambda: pool_vsum(pool, L1), lambda: None)

        @block.scalar
        def _(act):
            for c in range(4):
                act.dma_start(x[:, 8 * c:8 * c + 8, :], x_t[:, 8 * c:8 * c + 8, :]).then_inc(x_in[c], 16)
            act.dma_start(W1, W1_d).then_inc(consts_in, 16)
            act.dma_start(W2, W2_d).then_inc(consts_in, 16)
            act.dma_start(rhs1[:, 0:D], W3T_d).then_inc(consts_in, 16)
            act.dma_start(b3[:, :], pb3_d.partition_broadcast(P)).then_inc(consts_in, 16)
            act.wait_ge(pv_ready, 1)
            for c in range(NB):
                act.wait_ge(fbc_mm, c + 1)
                nc.scalar.activation(f1bc0[:, c * IB:(c + 1) * IB], bank[4 + c % 4][:, :], ACT.Identity,
                                     bias=pc[:, 0:1]).then_inc(fbc_ready, 1)
            act.wait_ge(fbc_ready, NB)

            def factored(L):
                scalar_weights(act, L)
                scalar_split(act, L)
                run_core(act, lambda b, g, f: scalar_unit(act, L, b, g, f), [])
                for k in range(KT):
                    scalar_evac(act, L, NB - 1, k)

            branch(act, L0, lambda: factored(L0), lambda: general_scalar(act, L0))
            for c in range(NB + 1):
                if c < NB:
                    act.wait_ge(trans_mm, c + 1)
                    nc.scalar.activation(featT[:, c * IB:(c + 1) * IB], bank[c % 2][:, :], ACT.Copy).then_inc(hT_ready, 1)
                for hh in range(2 if c else 0):
                    m = 2 * (c - 1) + hh
                    act.wait_ge(fbc_mm, NB + m + 1)
                    nc.scalar.activation(f1bc[hh][:, (c - 1) * IB:c * IB], bank[5 + m % 3][:, :], ACT.Identity,
                                         bias=pc[:, 2 + hh:3 + hh]).then_inc(fbc_ready, 1)
            act.wait_ge(fbc_ready, 3 * NB)
            branch(act, L1, lambda: factored(L1), lambda: general_scalar(act, L1))

        @block.vector
        def _(dve):
            count = [0]

            def link(ins):
                count[0] += 1
                ins.then_inc(dve_step, 1)
                dve.wait_ge(dve_step, count[0])

            nc.vector.memset(shift[:, 0:1], 4.0)
            nc.vector.memset(shift[:, 1:2], -2.0)
            link(nc.vector.memset(ones[:, :], 1.0))
            dve.wait_ge(consts_in, 16 * 10)
            dve.wait_ge(A_in, 64)
            for r in range(3):
                last = nc.vector.tensor_scalar(bb[:, r, :], ones[:, :], bcols[:, r:r + 1], None, ALU.mult)
            last.then_inc(bb_ready, 1)
            dve.wait_ge(pv_mm, 1)
            nc.vector.tensor_copy(pv[:, :], bank[0][:, 0:6])
            link(nc.vector.tensor_copy(pc[:, :], bank[1][:, 0:6]))
            nc.vector.tensor_tensor(pc[:, 0:2], pc[:, 0:2], b12[:, :], ALU.add)
            nc.vector.tensor_copy(rhs1[:, D:D + 4], pv[:, 2:6])
            for r, col in enumerate((0, 2, 3)):
                last = nc.vector.tensor_scalar(pvb[:, r, :], ones[:, :], pv[:, col:col + 1], None, ALU.mult)
            last.then_inc(pv_ready, 1)
            for c in range(5):
                if c < 4:
                    dve.wait_ge(x_in[c], 16)
                    nc.vector.memset(pause[:, :], 0.0)
                    ln_stats(dve, L0["ln0"], c, T // 4, c + 1, at=c * T // 4)
                if c >= 1:
                    ln_apply(dve, L0["ln0"], c - 1, T // 4, c, lambda t, n: vals[:, bass.ds(t, n), 0:D],
                             at=(c - 1) * T // 4)
            dve.wait_ge(pv_ready, 1)
            dve.wait_ge(fcol_mm, 1)
            f0 = bank[2][:, 0:2 * T].rearrange("p (t c) -> p t c", c=2)
            for c in range(2):
                last = nc.vector.tensor_scalar(fc[:, :, c], f0[:, :, c], pc[:, c:c + 1], None, ALU.add)
            last.then_inc(fc_ready, 1)
            dve.wait_ge(fc_ready, 1)
            nc.vector.memset(vals[:, :, D:D + 1], 1.0)
            vector_range(link, L0)

            def ln1_stats(b, step=None):
                ln_stats(dve, L0["ln1"], b, KT, b + 1)

            def ln1_apply(b):
                ln_apply(dve, L0["ln1"], b, KT, b + 1, lambda t, n: h[:, bass.ds(t, n), :])

            def result0(b):
                vector_result(dve, L0, b)
                dve.wait_ge(L0["x_done"], b + 1)
                nc.vector.memset(pause[:, :], 0.0)

            def core(L, after):
                vector_split(dve, L)
                dve.wait_ge(L["uv_set"], 1)
                run_core(dve, lambda b, g, f: vector_unit(dve, L, b, g, f),
                         [lambda b: vector_evac(dve, L, b), lambda b: vector_combine(dve, L, b)] + after)

            def factored0():
                before = count[0]
                vector_weights(link, L0)
                steps.append(count[0] - before)
                core(L0, [result0, ln1_stats, ln1_apply])

            def general0():
                general_vector(dve, L0)
                dve.sem_inc(dve_step, steps[0])
                with dve.Fori(0, NB) as b:
                    nc.vector.memset(pause[:, :], 0.0)
                    ln1_stats(b)
                    ln1_apply(b)

            steps = []
            branch(dve, L0, factored0, general0)

            v4 = vals3(L1)
            for c in range(NB):
                dve.wait_ge(v_mm, c + 1)
                src = bank[2 + c % 2][:, :].rearrange("p (t h w) -> p t h w", t=KT, h=2)
                bias = b3[:, :].rearrange("p (o h w) -> p o h w", o=1, h=2).broadcast_to([P, KT, 2, D // 2])
                nc.vector.memset(v4[:, KT * c:KT * c + KT, :, D // 2:D // 2 + 1], 1.0)
                nc.vector.tensor_tensor(v4[:, KT * c:KT * c + KT, :, 0:D // 2], src, bias, ALU.add).then_inc(v_ready, 1)
            f1p = bank[4][:, 0:4 * T].rearrange("p (t c) -> p t c", c=4)
            for c in range(4):
                last = nc.vector.tensor_scalar(fc[:, :, c], f1p[:, :, c], pc[:, 2 + c:3 + c], None, ALU.add)
            last.then_inc(fc_ready, 1)
            dve.wait_ge(fc_ready, 2)
            dve.wait_ge(v_ready, NB)
            link(nc.vector.tensor_reduce(st[:, 8:9], vals[:, :, :], AX.XY, ALU.max, apply_absolute_value=True))
            vector_range(link, L1)

            def factored1():
                vector_weights(link, L1)
                core(L1, [lambda b: vector_result(dve, L1, b)])

            branch(dve, L1, factored1, lambda: general_vector(dve, L1))

        @block.tensor
        def _(pe):
            pe.wait_ge(bb_ready, 1)
            rhs = (w12[:, :], A[:, 0:2], A[:, 2:4])
            for r, w in enumerate((W, W1, W2)):
                nc.tensor.matmul(bank[0][:, 2 * r:2 * r + 2], w, rhs[r], start=True, stop=True)
            for r in range(3):
                mm = nc.tensor.matmul(bank[1][:, 2 * r:2 * r + 2], bb[:, r, :], rhs[r], start=True, stop=True)
            mm.then_inc(pv_mm, 1)
            pe.wait_ge(pv_ready, 1)
            for t in range(T):
                if t % 8 == 0:
                    pe.wait_ge(feat_in[t // 8], 16)
                mm = nc.tensor.matmul(bank[2][:, 2 * t:2 * t + 2], featT[:, t * P:(t + 1) * P], pv[:, 0:2],
                                      start=True, stop=True)
            mm.then_inc(fcol_mm, 1)
            for c in range(NB):
                if c >= 4:
                    pe.wait_ge(fbc_ready, c - 3)
                nc.tensor.matmul(bank[4 + c % 4][:, :], pvb[:, 0, :], featT[:, c * IB:(c + 1) * IB],
                                 start=True, stop=True).then_inc(fbc_mm, 1)
            pe.wait_ge(fbc_ready, NB)
            pe.wait_ge(fc_ready, 1)

            def factored0():
                tensor_core(pe, L0)
                pe.wait_ge(L0["banks_free"], T)

            def general0():
                pe.wait_ge(L0["ln0"]["h_done"], 4)
                general_tensor(pe, L0)

            def project(c):
                pe.wait_ge(hT_ready, c + 1)
                if c >= 2:
                    pe.wait_ge(v_ready, c - 1)
                for j in range(KT):
                    t = KT * c + j
                    nc.tensor.matmul(bank[4][:, 4 * t:4 * t + 4], featT[:, t * P:(t + 1) * P], rhs1[:, D:D + 4],
                                     start=True, stop=True)
                    mm = nc.tensor.matmul(bank[2 + c % 2][:, j * D:(j + 1) * D], featT[:, t * P:(t + 1) * P], rhs1[:, 0:D],
                                          start=True, stop=True)
                mm.then_inc(v_mm, 1)
                for hh in range(2):
                    m = 2 * c + hh
                    if m >= 3:
                        pe.wait_ge(fbc_ready, NB + m - 2)
                    nc.tensor.matmul(bank[5 + m % 3][:, :], pvb[:, 1 + hh, :], featT[:, c * IB:(c + 1) * IB],
                                     start=True, stop=True).then_inc(fbc_mm, 1)

            pe.wait_ge(ident0, 4)
            branch(pe, L0, factored0, general0)
            for c in range(NB + 1):
                if c < NB:
                    pe.wait_ge(L0["ln1"]["h_done"], c + 1)
                    if c >= 2:
                        pe.wait_ge(hT_ready, c - 1)
                    for j in range(KT):
                        mm = nc.tensor.transpose(bank[c % 2][:, j * P:(j + 1) * P], h[:, KT * c + j, :], ident[:, :])
                    mm.then_inc(trans_mm, 1)
                if c >= 1:
                    project(c - 1)
            pe.wait_ge(fbc_ready, 3 * NB)
            pe.wait_ge(v_ready, NB)
            pe.wait_ge(fc_ready, 2)
            branch(pe, L1, lambda: tensor_core(pe, L1), lambda: general_tensor(pe, L1))


def kernel(x, adj, L0_gnn_inlayer2, L0_gnn_W, L0_gnn_b, L0_gnn_w1, L0_gnn_b1, L0_gnn_w2, L0_gnn_b2,
           L1_gnn_W1, L1_gnn_b1, L1_gnn_W2, L1_gnn_b2, L1_gnn_W3, L1_gnn_b3, L1_gnn_a):
    import numpy as np
    import concourse.bacc as bacc
    from concourse.bass_utils import run_bass_kernel_spmd

    nc = bacc.Bacc("TRN2", target_bir_lowering=False, num_devices=1)
    host = {
        "x": x, "adjT": np.asarray(adj).T, "adj": adj, "inlayer2T": np.asarray(L0_gnn_inlayer2).T,
        "W": L0_gnn_W, "b": L0_gnn_b, "w12": np.stack([np.asarray(L0_gnn_w1), np.asarray(L0_gnn_w2)], axis=1),
        "b12": np.concatenate([np.asarray(L0_gnn_b1), np.asarray(L0_gnn_b2)]),
        "W1": L1_gnn_W1, "W2": L1_gnn_W2, "W3T": np.asarray(L1_gnn_W3).T,
        "pb1": L1_gnn_b1, "pb2": L1_gnn_b2, "pb3": L1_gnn_b3, "a": L1_gnn_a,
    }
    arrays, args = {}, []
    for name, value in host.items():
        value = np.ascontiguousarray(value)
        arrays[f"in_{name}"] = value
        args.append(nc.dram_tensor(f"in_{name}", value.shape, mybir.dt.from_np(value.dtype), kind="ExternalInput").ap())
    args.append(nc.dram_tensor("result", (N, D), F32, kind="ExternalOutput").ap())
    gat_program(nc, *args)
    r = run_bass_kernel_spmd(nc, [arrays], core_ids=[0])
    return r.results[0]["result"]
```

```python
import concourse.bass as bass
from concourse import mybir
from concourse.alu_op_type import AluOpType as ALU
from contextlib import ExitStack

F32 = mybir.dt.float32
F16 = mybir.dt.float16
BF16 = mybir.dt.bfloat16
I32 = mybir.dt.int32
ACT = mybir.ActivationFunctionType
AX = mybir.AxisListType
RMAX = bass.bass_isa.ReduceOp.max

N = 4096
D = 128
P = 128
T = N // P
IB = 512
NB = N // IB
KT = IB // P
G = 4
NG = T // G
RAW = 4
LO = 2.0 ** 11
WSC = 2.0 ** 11
EPS = 1e-5
SPREAD = 16.0
LOGIT = 30.0
STEPS_AT = ((0, 0.5, 1, 1.5, 2, 3, 3.5, 4, 4.5, 5.5, 6), (0, 2, 2, 4, 4, 4))
LAG = 2
SLOT3 = (0, 1, 2, 0, 1, 2, 1, 2)
FIRST3 = (0, 1, 0, 1, 0, 2, 1, 2)
SLOT4 = (0, 1, 2, 3, 0, 1, 2, 3)
ACT_SIGNS = (1, 3)
SUMS_AT = (1, 1)
SIGN_LEAD = (1, 2)
VMAX = 31.0


def gat_program(nc, x_d, adjT_d, adj_d, x2T_d, W_d, b_d, w12_d, b12_d,
                W1_d, W2_d, W3T_d, pb1_d, pb2_d, pb3_d, a_d, out_d):
    ctx = ExitStack()
    with ctx:
        def sb(name, shape, dt=F32):
            return ctx.enter_context(nc.sbuf_tensor(name, shape, dt))

        def sem(name):
            return ctx.enter_context(nc.semaphore(name))

        x = sb("x", [P, T, D])
        featT = sb("featT", [P, N])
        f1bc0 = sb("f1bc0", [P, N])
        f1bc = (f1bc0, featT)
        raw = sb("raw", [P, RAW, G * IB], I32)
        q = sb("q", [P, 2, G * IB], BF16)
        s = sb("s", [P, 2, 2, G * IB], BF16)
        bc = sb("bc", [P, 2, 4, G * IB], BF16)
        vals = sb("vals", [P, T, 130])
        h = vals[:, :, 0:D]
        more = vals[:, :, :].rearrange("p t w -> p (t w)").bitcast(BF16)
        xy = sb("xy", [P, T * 520], F16)
        tb = sb("tb", [P, KT, 260])
        acc = sb("acc", [P, KT, 260])
        comb_fix = sb("comb_fix", [P, 2, KT, 130])
        comb, fix = comb_fix[:, 0], comb_fix[:, 1]
        prod = (tb[:, :, :].rearrange("p k w -> p (k w)"), acc[:, :, :].rearrange("p k w -> p (k w)"),
                comb_fix[:, :, :, :].rearrange("p f k w -> p (f k w)"))
        vsum = sb("vsum", [P, 130])
        ones = sb("ones", [P, P])
        ident = sb("ident", [P, P])
        early = bc[:, 0, 0:2, :].rearrange("p h i -> p (h i)").bitcast(F32)
        W, W1, W2 = (early[:, r * D:(r + 1) * D] for r in range(3))
        bb = early[:, 3 * D:6 * D].rearrange("p (r m) -> p r m", r=3)
        w3sq = early[:, 6 * D:7 * D]
        vbound = early[:, 7 * D:9 * D].rearrange("p (r m) -> p r m", r=2)
        room = early[:, 9 * D:10 * D]
        w3n = sb("w3n", [P, D])
        vmax2 = sb("vmax2", [P, 2])
        bcols = sb("bcols", [P, 3])
        w12 = sb("w12", [P, 2])
        A = sb("A", [P, 4])
        b12 = sb("b12", [P, 2])
        b3 = sb("b3", [P, D])
        pv = sb("pv", [P, 6])
        pc = sb("pc", [P, 6])
        pvb = sb("pvb", [P, P])
        rhs1 = sb("rhs1", [P, D + 4])
        fc = sb("fc", [P, T, 4])
        nfc = sb("nfc", [P, T, 4])
        shift = sb("shift", [P, 2])
        E = sb("E", [P, 2, T, 2])
        uv = sb("uv", [P, T, 2, 2])
        uvt = sb("uvt", [P, 4, T, 2])
        uvcur = sb("uvcur", [P, KT, 2, 2])
        st = sb("st", [P, 10])
        sta = sb("sta", [P, 10])
        ng = sb("ng", [P, 4])
        nz = sb("nz", [P, KT, 2])
        rden = sb("rden", [P, KT, 2])
        bst = sb("bst", [P, T, 6])
        bag = sb("bag", [P, T, 2])
        vare = sb("vare", [P, T])
        pause = sb("pause", [P, 1])
        flag = sb("flag", [P, 2], I32)
        am = sb("am", [P, 4])
        ok = sb("ok", [P, 8])
        nmax = sb("nmax", [P, 1])
        rsum = sb("rsum", [P, 2])
        gadj = bc[:, 0, :, :].rearrange("p k i -> p (k i)").bitcast(I32)[:, 0:N]
        gneg = bc[:, 0, :, :].rearrange("p k i -> p (k i)").bitcast(F32)[:, 0:N]
        glog = bc[:, 1, :, :].rearrange("p k i -> p (k i)").bitcast(F32)[:, 0:N]
        gT = s[:, :, :, :].rearrange("p k h i -> p (k h i)").bitcast(F32)[:, 0:N]
        gf2 = xy[:, :].bitcast(F32)[:, 0:N]
        gcol = fix[:, :, :].rearrange("p k w -> p (k w)")[:, 0:P]
        mhalf = sb("mhalf", [P, T])
        rstd = sb("rstd", [P, T])
        nmr = sb("nmr", [P, T])
        ft = sb("ft", [P, 2, T])
        fT = sb("fT", [2 * T, P])

        bank = [ctx.enter_context(nc.psum_tensor(f"bank{i}", [P, 512], F32)) for i in range(8)]

        LAY = [dict(i=0, H=1, Wd=129, slope=0.01, logit=LOGIT, sign=1.0), dict(i=1, H=2, Wd=65, slope=0.2, logit=1e30, sign=-1.0)]
        for L in LAY:
            i = L["i"]
            L["adj_in"] = [sem(f"adj_in{i}_{r}") for r in range(RAW)]
            for name in ("q_ready", "s_ready", "t_ready", "g_ready", "bc_ready", "bc_used", "tiles_done",
                         "uv_ready", "b_scaled", "banks_free", "comb_done", "nz_done", "fix_done", "sum_done",
                         "rden_done", "x_done", "stat", "allmax", "g_max", "exp_done", "uvp", "uv_exp", "uv_set", "e_ready",
                         "flag_ready", "gen_adj_in", "gen_col", "gen_mm", "gen_row", "gen_logit", "gen_exp", "gen_tr",
                         "gen_pt", "gen_sum", "gen_rec", "gen_free", "gen_step",
                         "prod_done", "hi_done", "xy_ready", "vsum_mm", "vsum_ready"):
                L[name] = sem(f"{name}{i}")
        for ln in ("ln0", "ln1"):
            LAY[0][ln] = {name: sem(f"{ln}_{name}") for name in ("bst_done", "bag_done", "var_done", "rstd_done", "norm_done", "h_done")}
        x_in = [sem(f"x_in{c}") for c in range(4)]
        feat_in = [sem(f"feat_in{c}") for c in range(4)]
        first_in = sem("first_in")
        consts_in = sem("consts_in")
        A_in = sem("A_in")
        ident0 = sem("ident0")
        bb_ready = sem("bb_ready")
        pv_mm = sem("pv_mm")
        pv_ready = sem("pv_ready")
        fcol_mm = sem("fcol_mm")
        fbc_mm = sem("fbc_mm")
        fbc_ready = sem("fbc_ready")
        ft_ready, ft_mm, fT_ready, f1_out = sem("ft_ready"), sem("ft_mm"), sem("fT_ready"), sem("f1_out")
        f1_in = [sem("f1_in0"), sem("f1_in1")]
        fc_ready = sem("fc_ready")
        trans_mm = sem("trans_mm")
        hT_ready = sem("hT_ready")
        v_mm = sem("v_mm")
        v_ready = sem("v_ready")
        dve_step = sem("dve_step")
        out_done = sem("out_done")

        x_t = x_d.rearrange("(t p) d -> p t d", p=P)
        out_t = out_d.rearrange("(t p) d -> p t d", p=P)
        adjT_t = adjT_d.rearrange("(t p) i -> p t i", p=P)

        def xy5(L):
            H, Wd = L["H"], L["Wd"]
            return xy[:, 0:T * H * 4 * Wd].rearrange("p (t h k r w) -> p t h k r w", h=H, k=2, r=2, w=Wd)

        def vals3(L):
            return vals[:, :, 0:L["H"] * L["Wd"]].rearrange("p t (h w) -> p t h w", h=L["H"])

        def slots(L, first):
            return FIRST3 if L["i"] == 1 and first else SLOT3

        def qs_slots(L, first):
            return SLOT4 if L["i"] == 0 else slots(L, first)

        def since(order, L, g, first):
            slot = order(L, first)[g]
            for d in range(1, g + 1 if first else NG + 1):
                if d <= g:
                    used = order(L, first)[g - d] == slot
                else:
                    used = slot in (order(L, False)[g - d + NG], order(L, True)[g - d + NG])
                if used:
                    return d
            return None

        def piece(m):
            return more[:, m * G * IB:(m + 1) * G * IB]

        def q_of(L, g, first):
            return (q[:, 0, :], q[:, 1, :], bc[:, 0, 3, :], bc[:, 1, 3, :])[qs_slots(L, first)[g]]

        def s_of(L, g, hh, first):
            if L["i"] == 0:
                return s[:, SLOT4[g] // 2, SLOT4[g] % 2, :]
            return (s[:, 0, hh, :], s[:, 1, hh, :], (bc[:, 1, 3, :], piece(3))[hh])[qs_slots(L, first)[g]]

        def m_of(L, g, m, first):
            slot = slots(L, first)[g]
            if slot < 2:
                return bc[:, slot, m, :]
            return bc[:, m, 2, :] if L["i"] == 0 else piece(m)

        def load_unit(sp, L, b, g, first):
            if not first:
                sp.wait_ge(L["q_ready"], NG * b + g - RAW + 1)
            sp.dma_start(raw[:, g % RAW, :].rearrange("p (t i) -> p t i", t=G),
                         adjT_t[:, G * g:G * g + G, bass.ds(b * IB, IB)]).then_inc(L["adj_in"][g % RAW], 16)

        def act_jts(L, g, first):
            if L["i"] == 0:
                return [(j, 0) for j in range(ACT_SIGNS[0] if g == SUMS_AT[0] and not first else ACT_SIGNS[1])]
            return [(j, hh) for hh in range(2) for j in range(G) if hh == 0 or j == 0]

        def dve_jts(L, g, first):
            return [(j, hh) for hh in range(L["H"]) for j in range(G) if (j, hh) not in act_jts(L, g, first)]

        def scalar_edges(act, L, b, g, first):
            n, ago = NG * b + g, since(qs_slots, L, g, first)
            if ago:
                act.wait_ge(L["bc_ready"], n - ago + 1)
            act.wait_ge(L["adj_in"][g % RAW], 16 * (2 * b + g // RAW + 1))
            if L["i"] == 0:
                nc.scalar.activation(q_of(L, g, first), raw[:, g % RAW, :], ACT.Relu, bias=shift[:, 0:1],
                                     scale=-4.0).then_inc(L["q_ready"], 1)
            else:
                nc.scalar.activation(q_of(L, g, first), raw[:, g % RAW, :], ACT.Square, bias=shift[:, 1:2],
                                     scale=2.0).then_inc(L["q_ready"], 1)

        def scalar_signs(L, b, g, first, begin, end):
            signs = act_jts(L, g, first)
            for m in range(begin, min(end, len(signs))):
                j, hh = signs[m]
                src = nfc if L["i"] == 0 else fc
                last = nc.scalar.activation(s_of(L, g, hh, first)[:, j * IB:(j + 1) * IB], f1bc[hh][:, bass.ds(b * IB, IB)],
                                            ACT.Sign, bias=src[:, G * g + j, L["H"] + hh:L["H"] + hh + 1],
                                            scale=-1.0 if L["i"] == 0 else 1.0)
                if m == len(signs) - 1:
                    last.then_inc(L["s_ready"], 1)

        def scalar_unit(act, L, b, g, first=False):
            scalar_edges(act, L, b, g, first)
            if g == SUMS_AT[L["i"]] and not first:
                lead = SIGN_LEAD[L["i"]]
                scalar_signs(L, b, g, first, 0, lead)
                for k in range(KT):
                    scalar_evac(act, L, b - 1, k)
                    scalar_signs(L, b, g, first, lead + k, lead + k + 1 if k < KT - 1 else 2 * G)
            else:
                scalar_signs(L, b, g, first, 0, 2 * G)

        def bc_free(dve, L, b, g, first):
            ago = since(slots, L, g, first)
            if not ago:
                return
            last = g - ago
            if last % NG == NG - 1:
                dve.wait_ge(L["tiles_done"], KT * b)
            elif last < 0:
                dve.wait_ge(L["bc_used"], (NG - 1) * b + last + 2)
            else:
                dve.wait_ge(L["bc_used"], (NG - 1) * b + last + 1)

        def vector_signs(dve, L, b, g, first):
            ago = since(qs_slots, L, g, first)
            if ago:
                dve.wait_ge(L["bc_ready"], NG * b + g - ago + 1)
            for j, hh in dve_jts(L, g, first):
                dst, f1 = s_of(L, g, hh, first)[:, j * IB:(j + 1) * IB], f1bc[hh][:, bass.ds(b * IB, IB)]
                nf2 = nfc[:, G * g + j, L["H"] + hh:L["H"] + hh + 1]
                if L["i"] == 0:
                    last = nc.vector.tensor_scalar(dst, f1, nf2, None, ALU.is_lt)
                else:
                    last = nc.vector.tensor_scalar(dst, f1, nf2, -1.0, ALU.is_ge, ALU.add)
            last.then_inc(L["t_ready"], 1)

        def vector_unit(dve, L, b, g, first, within=lambda: None):
            n, each = NG * b + g, L["i"] == 1 and first
            if g == 0 or each:
                vector_signs(dve, L, b, g, first)
            dve.wait_ge(L["q_ready"], n + 1)
            if L["i"] == 0:
                dve.wait_ge(L["s_ready"], n + 1)
                dve.wait_ge(L["t_ready"], n + 1)
                nc.vector.tensor_tensor(s_of(L, g, 0, first), s_of(L, g, 0, first), q_of(L, g, first), ALU.add).then_inc(L["g_ready"], 1)
                if g < NG - 1 and not each:
                    vector_signs(dve, L, b, g + 1, first)
                within()
                dve.wait_ge(L["g_ready"], n + 1)
                bc_free(dve, L, b, g, first)
                nc.vector.tensor_scalar(m_of(L, g, 0, first), s_of(L, g, 0, first), 0.0, None, ALU.is_le)
                nc.vector.tensor_scalar(m_of(L, g, 1, first), s_of(L, g, 0, first), 1.0, None,
                                        ALU.is_equal).then_inc(L["bc_ready"], 1)
            else:
                bc_free(dve, L, b, g, first)
                nc.vector.tensor_scalar(m_of(L, g, 2, first), q_of(L, g, first), 0.0, -1.0, ALU.is_equal, ALU.mult)
                dve.wait_ge(L["s_ready"], n + 1)
                dve.wait_ge(L["t_ready"], n + 1)
                nc.vector.tensor_tensor(m_of(L, g, 0, first), q_of(L, g, first), s_of(L, g, 0, first), ALU.is_le)
                nc.vector.tensor_tensor(m_of(L, g, 1, first), q_of(L, g, first), s_of(L, g, 1, first),
                                        ALU.is_le).then_inc(L["bc_ready"], 1)
                if g < NG - 1 and not each:
                    vector_signs(dve, L, b, g + 1, first)

        def tensor_unit(pe, L, b, g, first):
            H, Wd = L["H"], L["Wd"]
            v = xy5(L)
            if first:
                pe.wait_ge(L["xy_ready"], g + 1)
            pe.wait_ge(L["bc_ready"], NG * b + g + 1)
            for k in range(KT):
                if g == 0 and not first:
                    pe.wait_ge(L["banks_free"], KT * b - KT + k + 1)
                for j in range(G):
                    t, begin, end = G * g + j, g == 0 and j == 0, g == NG - 1 and j == G - 1
                    c = slice(j * IB + k * P, j * IB + (k + 1) * P)
                    if L["i"] == 0:
                        for kind in range(2):
                            mm = nc.tensor.matmul(bank[2 * k + kind][:, 0:2 * Wd], m_of(L, g, kind, first)[:, c], v[:, t, 0, kind, :, :],
                                                  start=begin, stop=end)
                    else:
                        for hh in range(2):
                            nc.tensor.matmul(bank[2 * k + hh][:, 0:4 * Wd], m_of(L, g, hh, first)[:, c],
                                             v[:, t, hh, :, :, :], start=begin, stop=end,
                                             skip_group_check=True)
                            mm = nc.tensor.matmul(bank[2 * k + hh][:, 2 * Wd:4 * Wd], m_of(L, g, 2, first)[:, c],
                                                  v[:, t, hh, 1, :, :], start=False, stop=end, skip_group_check=True)
                if g == NG - 1:
                    mm.then_inc(L["tiles_done"], 1)
            if g < NG - 1:
                mm.then_inc(L["bc_used"], 1)

        def tensor_core(pe, L):
            for g in range(NG):
                tensor_unit(pe, L, 0, g, True)
            with pe.Fori(1, NB) as b:
                for g in range(NG):
                    tensor_unit(pe, L, b, g, False)

        def sums(L, k, hh):
            Wd = L["Wd"]
            if L["i"] == 0:
                return bank[2 * k][:, 0:2 * Wd], bank[2 * k + 1][:, 0:2 * Wd]
            return bank[2 * k + hh][:, 0:2 * Wd], bank[2 * k + hh][:, 2 * Wd:4 * Wd]

        def scalar_evac(act, L, b, k):
            H, Wd = L["H"], L["Wd"]
            if k == 0:
                act.wait_ge(L["uv_ready"], b + 1)
            act.wait_ge(L["tiles_done"], KT * b + k + 1)
            for hh in range(H):
                last = nc.scalar.activation(tb[:, k, hh * 2 * Wd:(hh + 1) * 2 * Wd], sums(L, k, hh)[0], ACT.Copy,
                                            scale=uvcur[:, k, 0, hh:hh + 1])
            last.then_inc(L["b_scaled"], 1)

        def vector_factors(dve, L, b):
            H = L["H"]
            nc.vector.tensor_scalar(uvcur[:, :, :, 0:H], uv[:, bass.ds(b * KT, KT), :, 0:H], 1.0, None,
                                    ALU.mult).then_inc(L["uv_ready"], 1)

        def vector_evac(dve, L, b):
            H, Wd = L["H"], L["Wd"]
            dve.wait_ge(L["uv_ready"], b + 1)
            for k in range(KT):
                dve.wait_ge(L["b_scaled"], KT * b + k + 1)
                for hh in range(H):
                    c = slice(hh * 2 * Wd, (hh + 1) * 2 * Wd)
                    last = nc.vector.scalar_tensor_tensor(out=acc[:, k, c], in0=sums(L, k, hh)[1],
                                                          scalar=uvcur[:, k, 1, hh:hh + 1], in1=tb[:, k, c],
                                                          op0=ALU.mult, op1=ALU.add)
                last.then_inc(L["banks_free"], 1)

        def vector_combine(dve, L, b):
            H, Wd = L["H"], L["Wd"]
            CW = H * Wd
            dve.wait_ge(L["banks_free"], KT * b + KT)
            a5 = acc[:, :, 0:2 * CW].rearrange("p k (h r w) -> p k h r w", h=H, r=2)
            nc.vector.tensor_scalar(nz[:, :, 0:H], a5[:, :, :, 0, Wd - 1], 0.0, None, ALU.is_equal).then_inc(L["nz_done"], 1)
            a4 = acc[:, :, 0:2 * CW].rearrange("p k (h r w) -> p (k h) r w", h=H, r=2)
            c3 = comb[:, :, 0:CW].rearrange("p k (h w) -> p (k h) w", h=H)
            nc.vector.scalar_tensor_tensor(out=c3, in0=a4[:, :, 1, :], scalar=1.0 / LO, in1=a4[:, :, 0, :],
                                           op0=ALU.mult, op1=ALU.add).then_inc(L["comb_done"], 1)

        def vector_fix(dve, L, b):
            H, Wd = L["H"], L["Wd"]
            f4 = fix[:, :, 0:H * Wd].rearrange("p k (h w) -> p k h w", h=H)
            dve.wait_ge(L["nz_done"], b + 1)
            dve.wait_ge(L["vsum_ready"], 1)
            vs = vsum[:, 0:H * Wd].rearrange("p (o h w) -> p o h w", o=1, h=H).broadcast_to([P, KT, H, Wd])
            nc.vector.tensor_tensor(f4, vs, nz[:, :, 0:H].unsqueeze(3).broadcast_to([P, KT, H, Wd]),
                                    ALU.mult).then_inc(L["fix_done"], 1)

        def vector_sum(dve, L, b):
            CW = L["H"] * L["Wd"]
            dve.wait_ge(L["comb_done"], b + 1)
            dve.wait_ge(L["fix_done"], b + 1)
            nc.vector.tensor_tensor(fix[:, :, 0:CW], comb[:, :, 0:CW], fix[:, :, 0:CW], ALU.add).then_inc(L["sum_done"], 1)

        def vector_rden(dve, L, b):
            H, Wd = L["H"], L["Wd"]
            f4 = fix[:, :, 0:H * Wd].rearrange("p k (h w) -> p k h w", h=H)
            dve.wait_ge(L["sum_done"], b + 1)
            nc.vector.reciprocal(rden[:, :, 0:H], f4[:, :, :, Wd - 1]).then_inc(L["rden_done"], 1)

        def vector_result(dve, L, b):
            H, w = L["H"], L["Wd"] - 1
            f4 = fix[:, :, 0:H * L["Wd"]].rearrange("p k (h w) -> p k h w", h=H)
            dve.wait_ge(L["rden_done"], b + 1)
            for k in range(KT):
                for hh in range(H):
                    xs = x[:, bass.ds(b * KT + k, 1), hh * w:(hh + 1) * w].rearrange("p o w -> p (o w)")
                    last = nc.vector.scalar_tensor_tensor(out=xs, in0=f4[:, k, hh, 0:w], scalar=rden[:, k, hh:hh + 1],
                                                          in1=xs, op0=ALU.mult, op1=ALU.add)
            last.then_inc(L["x_done"], 1)

        def ln_stats(L, b, tiles, at=0):
            for k in range(tiles):
                last = nc.vector.bn_stats(bst[:, at + k, :], x[:, bass.ds(b * tiles + k, 1), :].rearrange("p o w -> p (o w)"))
            last.then_inc(L["bst_done"], 1)

        def ln_mean(dve, L, tiles, step, at=0):
            dve.wait_ge(L["bst_done"], step)
            nc.vector.memset(pause[:, :], 0.0)
            for k in range(tiles):
                last = nc.vector.bn_aggr(bag[:, at + k, :], bst[:, at + k, :])
            last.then_inc(L["bag_done"], 1)

        def ln_var(dve, L, tiles, step, at=0):
            dve.wait_ge(L["bag_done"], step)
            nc.vector.tensor_scalar(vare[:, at:at + tiles], bag[:, at:at + tiles, 1], EPS, None, ALU.add).then_inc(L["var_done"], 1)

        def ln_norm(dve, L, b, step):
            dve.wait_ge(L["rstd_done"], step)
            for k in range(KT):
                last = nc.vector.tensor_scalar(h[:, bass.ds(b * KT + k, 1), :], x[:, bass.ds(b * KT + k, 1), :],
                                               bag[:, k, 0:1], rstd[:, k:k + 1], ALU.subtract, ALU.mult)
            last.then_inc(L["norm_done"], 1)

        def ln_relu(dve, L, b, step):
            dve.wait_ge(L["norm_done"], step)
            hb = h[:, bass.ds(b * KT, KT), :]
            nc.vector.tensor_scalar(hb, hb, 0.0, None, ALU.max).then_inc(L["h_done"], 1)

        def pool_rstd(pool, L, tiles, step, at=0):
            pool.wait_ge(L["var_done"], step)
            nc.gpsimd.tensor_tensor(rstd[:, at:at + tiles], vare[:, at:at + tiles], mhalf[:, at:at + tiles], ALU.pow).then_inc(L["rstd_done"], 1)

        def run_core(eng, first, unit, before, after, at, rest=lambda: None, end={}):
            first()
            rest()
            with eng.Fori(1, NB) as b:
                for step in before:
                    step(b - 1)
                for g in range(NG):
                    unit(b, g, False)
                    for m in range(len(at)):
                        if at[m] == g:
                            after[m](b - 1)
            for step in before:
                step(NB - 1)
            for m, step in enumerate(after):
                step(NB - 1)
                if m in end:
                    end[m]()

        def vector_range(link, L):
            H = L["H"]
            link(nc.vector.tensor_scalar(nfc[:, :, 0:2 * H], fc[:, :, 0:2 * H], -1.0, None, ALU.mult))
            nc.vector.tensor_reduce(st[:, 0:2 * H], fc[:, :, 0:2 * H].rearrange("p t c -> p c t"), AX.X, ALU.max)
            link(nc.vector.tensor_reduce(st[:, 2 * H:4 * H], nfc[:, :, 0:2 * H].rearrange("p t c -> p c t"), AX.X, ALU.max))
            nc.vector.sem_inc(L["stat"], 1)

        def vector_flag(link, L):
            H = L["H"]
            nc.vector.tensor_tensor(am[:, 0:2 * H], sta[:, 0:2 * H], sta[:, 2 * H:4 * H], ALU.max)
            link(nc.vector.tensor_tensor(ok[:, 0:H], sta[:, H:2 * H], sta[:, 3 * H:4 * H], ALU.add))
            nc.vector.tensor_scalar(ok[:, 0:H], ok[:, 0:H], SPREAD, None, ALU.is_le)
            link(nc.vector.tensor_tensor(ok[:, H:2 * H], am[:, 0:H], am[:, H:2 * H], ALU.add))
            link(nc.vector.tensor_scalar(ok[:, H:2 * H], ok[:, H:2 * H], L["logit"], None, ALU.is_le))
            if L["i"] == 0:
                last = nc.vector.tensor_tensor(flag[:, 0:1], ok[:, 0:1], ok[:, 1:2], ALU.mult)
            else:
                nc.vector.tensor_scalar(ok[:, 4:6], vmax2[:, :], 0.0, None, ALU.is_le)
                link(nc.vector.tensor_tensor(ok[:, 0:2], ok[:, 0:2], ok[:, 2:4], ALU.mult))
                link(nc.vector.tensor_tensor(ok[:, 0:2], ok[:, 0:2], ok[:, 4:6], ALU.mult))
                last = nc.vector.tensor_tensor(flag[:, 1:2], ok[:, 0:1], ok[:, 1:2], ALU.mult)
            last.then_inc(L["flag_ready"], 1)

        def vector_weights(link, L):
            H, a = L["H"], L["slope"]
            nc.vector.wait_ge(L["allmax"], 1)
            link(nc.vector.tensor_scalar(ng[:, 0:H], sta[:, H:2 * H], -1.0, None, ALU.mult))
            nc.vector.tensor_scalar(ng[:, 2:2 + H], sta[:, H:2 * H], -a, None, ALU.mult).then_inc(L["g_max"], 1)
            for hh in range(H):
                last = nc.vector.tensor_scalar(uvt[:, 0, :, hh], fc[:, :, hh], sta[:, H + hh:H + hh + 1], None, ALU.add)
            link(last)
            y, m = uvt[:, 0, :, 0:H], uvt[:, 1, :, 0:H]
            link(nc.vector.scalar_tensor_tensor(out=m, in0=y, scalar=a, in1=y, op0=ALU.mult, op1=ALU.max))
            nc.vector.tensor_tensor(uvt[:, 2, :, 0:H], y, m, ALU.subtract)
            nc.vector.scalar_tensor_tensor(out=uvt[:, 3, :, 0:H], in0=y, scalar=a, in1=m, op0=ALU.mult,
                                           op1=ALU.subtract).then_inc(L["uvp"], 1)

        def vector_scale(L):
            H = L["H"]
            nc.vector.wait_ge(L["exp_done"], 1)
            nc.vector.tensor_scalar(E[:, :, :, 0:H], E[:, :, :, 0:H], WSC * LO, None, ALU.mult).then_inc(L["e_ready"], 1)
            nc.vector.wait_ge(L["uv_exp"], 1)
            nc.vector.tensor_scalar(uv[:, :, 1, 0:H], uv[:, :, 1, 0:H], L["sign"], None, ALU.mult).then_inc(L["uv_set"], 1)
            nc.vector.wait_ge(L["e_ready"], 1)
            nc.vector.wait_ge(L["uv_set"], 1)

        def scalar_weights(act, L):
            H, a = L["H"], L["slope"]
            act.wait_ge(L["g_max"], 1)
            for hh in range(H):
                nc.scalar.activation(E[:, 0, :, hh], fc[:, :, H + hh], ACT.Exp, bias=ng[:, hh:hh + 1], scale=1.0)
                last = nc.scalar.activation(E[:, 1, :, hh], fc[:, :, H + hh], ACT.Exp, bias=ng[:, 2 + hh:3 + hh], scale=a)
            last.then_inc(L["exp_done"], 1)
            act.wait_ge(L["uvp"], 1)
            for r in range(2):
                last = nc.scalar.activation(uv[:, :, r, 0:H], uvt[:, 2 + r, :, 0:H], ACT.Exp)
            last.then_inc(L["uv_exp"], 1)

        def product(L, g):
            return prod[g % 3][:, 0:2 * G * L["H"] * L["Wd"]].rearrange("p (m w) -> p m w", w=L["Wd"])

        def part(L, g, r):
            return xy5(L)[:, G * g:G * g + G, :, :, r, :].rearrange("p t h k w -> p (t h k) w")

        def vector_split(dve, L, g):
            H, Wd = L["H"], L["Wd"]
            if g < NG:
                if L["i"] == 0 and g % 2 == 0:
                    dve.wait_ge(L["ln0"]["h_done"], g // 2 + 1)
                if g >= 3:
                    dve.wait_ge(L["xy_ready"], g - 2)
                v = vals[:, G * g:G * g + G, 0:H * Wd].rearrange("p t (h w) -> p (t h) w", h=H)
                e = E[:, :, G * g:G * g + G, 0:H].rearrange("p k t h -> p (t h) k")
                nc.vector.tensor_tensor(product(L, g).rearrange("p (m k) w -> p m k w", k=2),
                                        v.unsqueeze(2).broadcast_to([P, G * H, 2, Wd]),
                                        e.unsqueeze(3).broadcast_to([P, G * H, 2, Wd]),
                                        ALU.mult).then_inc(L["prod_done"], 1)
            if g >= LAG:
                dve.wait_ge(L["hi_done"], g - LAG + 1)
                nc.vector.scalar_tensor_tensor(out=part(L, g - LAG, 1), in0=part(L, g - LAG, 0), scalar=-LO,
                                               in1=product(L, g - LAG), op0=ALU.mult,
                                               op1=ALU.add).then_inc(L["xy_ready"], 1)

        def scalar_split(act, L, g):
            act.wait_ge(L["prod_done"], g + 1)
            nc.scalar.activation(part(L, g, 0), product(L, g), ACT.Copy, scale=1.0 / LO).then_inc(L["hi_done"], 1)

        def tensor_vsum(pe, L, tiles):
            CW = L["H"] * L["Wd"]
            for t in tiles:
                mm = nc.tensor.matmul(bank[3][:, 0:CW], ones[:, :], vals[:, t, 0:CW], start=t == 0, stop=t == T - 1)
            return mm

        def scalar_vsum(act, L):
            CW = L["H"] * L["Wd"]
            act.wait_ge(L["vsum_mm"], 1)
            nc.scalar.activation(vsum[:, 0:CW], bank[3][:, 0:CW], ACT.Copy).then_inc(L["vsum_ready"], 1)

        def pool_stats(pool, L, cols):
            pool.wait_ge(L["stat"], 1)
            nc.gpsimd.partition_all_reduce(sta[:, 0:cols], st[:, 0:cols], P, RMAX).then_inc(L["allmax"], 1)

        def branch(eng, L, factored, general):
            eng.wait_ge(L["flag_ready"], 1)
            holds = eng.value_load(flag[0:1, L["i"]:L["i"] + 1], min_val=0, max_val=1)
            with eng.If(holds != 0):
                factored()
            with eng.Else():
                general()

        def general_sync(sp, L):
            for r in range(RAW):
                sp.wait_ge(L["adj_in"][r], 16)
            for hh in range(L["H"]):
                with sp.Fori(0, T) as t:
                    sp.wait_ge(L["gen_free"], hh * T + t + 1)
                    sp.dma_start(gadj, adj_d.rearrange("(t p) j -> p t j", p=P)[:, bass.ds(t, 1), :]
                                 .rearrange("p o j -> p (o j)")).then_inc(L["gen_adj_in"], 16)

        def general_vector(dve, L):
            H, Wd = L["H"], L["Wd"]
            w = Wd - 1
            dve.sem_inc(L["gen_free"], 1)
            for hh in range(H):
                with dve.Fori(0, T) as t:
                    n = hh * T + t
                    nc.vector.tensor_scalar(gcol, ones[:, :], fc[:, bass.ds(t, 1), H + hh], None,
                                            ALU.mult).then_inc(L["gen_col"], 1)
                    dve.wait_ge(L["gen_mm"], n + 1)
                    nc.vector.tensor_scalar(gf2[:, bass.ds(t * P, P)], bank[0][:, 0:P], 1.0, None,
                                            ALU.mult).then_inc(L["gen_row"], 1)
                dve.wait_ge(L["gen_row"], hh * T + T)
                with dve.Fori(0, T) as t:
                    n = hh * T + t
                    step = 4 * n
                    dve.wait_ge(L["gen_adj_in"], 16 * n + 16)
                    nc.vector.tensor_scalar(glog, gf2, fc[:, bass.ds(t, 1), hh], None, ALU.add).then_inc(L["gen_step"], 1)
                    dve.wait_ge(L["gen_step"], step + 1)
                    nc.vector.scalar_tensor_tensor(out=glog, in0=glog, scalar=L["slope"], in1=glog, op0=ALU.mult,
                                                   op1=ALU.max).then_inc(L["gen_step"], 1)
                    dve.wait_ge(L["gen_step"], step + 2)
                    if L["i"] == 0:
                        nc.vector.tensor_scalar(gneg, gadj, 0.0, -1e9, ALU.is_le, ALU.mult).then_inc(L["gen_step"], 1)
                    else:
                        nc.vector.scalar_tensor_tensor(out=glog, in0=gadj, scalar=1.0, in1=glog, op0=ALU.is_equal,
                                                       op1=ALU.mult)
                        nc.vector.tensor_scalar(gneg, gadj, 1.0, -9e15, ALU.not_equal, ALU.mult).then_inc(L["gen_step"], 1)
                    dve.wait_ge(L["gen_step"], step + 3)
                    nc.vector.tensor_tensor(glog, glog, gneg, ALU.add).then_inc(L["gen_step"], 1)
                    dve.wait_ge(L["gen_step"], step + 4)
                    nc.vector.tensor_reduce(nmax[:, :], glog, AX.X, ALU.max, negate=True).then_inc(L["gen_logit"], 1)
                    dve.wait_ge(L["gen_exp"], n + 1)
                    nc.vector.reciprocal(rsum[:, 1:2], rsum[:, 0:1]).then_inc(L["gen_rec"], 1)
                    dve.wait_ge(L["gen_rec"], n + 1)
                    dve.wait_ge(L["gen_sum"], n + 1)
                    xs = x[:, bass.ds(t, 1), hh * w:(hh + 1) * w].rearrange("p o w -> p (o w)")
                    nc.vector.scalar_tensor_tensor(out=xs, in0=bank[2][:, 0:w], scalar=rsum[:, 1:2], in1=xs,
                                                   op0=ALU.mult, op1=ALU.add).then_inc(L["gen_free"], 1)
            dve.wait_ge(L["gen_free"], H * T + 1)

        def general_scalar(act, L):
            for hh in range(L["H"]):
                with act.Fori(0, T) as t:
                    n = hh * T + t
                    act.wait_ge(L["gen_logit"], n + 1)
                    nc.scalar.activation(glog, glog, ACT.Exp, bias=nmax[:, 0:1], scale=1.0,
                                         accum_out=rsum[:, 0:1]).then_inc(L["gen_exp"], 1)
                    for c in range(NB):
                        act.wait_ge(L["gen_tr"], NB * n + c + 1)
                        nc.scalar.activation(gT[:, c * IB:(c + 1) * IB], bank[c % 2][:, :],
                                             ACT.Copy).then_inc(L["gen_pt"], 1)

        def general_tensor(pe, L):
            for hh in range(L["H"]):
                with pe.Fori(0, T) as t:
                    pe.wait_ge(L["gen_col"], hh * T + t + 1)
                    nc.tensor.matmul(bank[0][:, 0:P], gcol, ident[:, :], start=True, stop=True).then_inc(L["gen_mm"], 1)
                pe.wait_ge(L["gen_row"], hh * T + T)
                with pe.Fori(0, T) as t:
                    n = hh * T + t
                    pe.wait_ge(L["gen_exp"], n + 1)
                    for c in range(NB):
                        if c >= 2:
                            pe.wait_ge(L["gen_pt"], NB * n + c - 1)
                        for j in range(4):
                            k = 4 * c + j
                            mm = nc.tensor.transpose(bank[c % 2][:, j * P:(j + 1) * P], glog[:, k * P:(k + 1) * P],
                                                     ident[:, :])
                        mm.then_inc(L["gen_tr"], 1)
                    pe.wait_ge(L["gen_pt"], NB * n + NB)
                    for j in range(T):
                        mm = nc.tensor.matmul(bank[2][:, 0:L["Wd"] - 1], gT[:, j * P:(j + 1) * P],
                                              vals3(L)[:, j, hh, 0:L["Wd"] - 1], start=(j == 0), stop=(j == T - 1))
                    mm.then_inc(L["gen_sum"], 1)
            pe.wait_ge(L["gen_free"], L["H"] * T + 1)

        f1_rows = nc.dram_tensor("f1_rows", (2 * T, P), F32, kind="Internal").ap()

        block = ctx.enter_context(nc.Block())
        L0, L1 = LAY

        def rows_of_block0(eng):
            eng.wait_ge(f1_in[0], 32)

        def rows_of_others(eng):
            eng.wait_ge(f1_in[1], 32)

        @block.sync
        def _(sp):
            sp.dma_start(W, W_d).then_inc(first_in, 16)
            sp.dma_start(w12[:, :], w12_d).then_inc(first_in, 16)
            sp.dma_start(bcols[:, 0:1], b_d.unsqueeze(1)).then_inc(first_in, 16)
            sp.dma_start(b12[:, :], b12_d.partition_broadcast(P)).then_inc(first_in, 16)
            for c in range(4):
                sp.dma_start(featT[:, c * 1024:(c + 1) * 1024], x2T_d[:, c * 1024:(c + 1) * 1024]).then_inc(feat_in[c], 16)
            sp.dma_start(bcols[:, 1:2], pb1_d.unsqueeze(1)).then_inc(consts_in, 16)
            sp.dma_start(bcols[:, 2:3], pb2_d.unsqueeze(1)).then_inc(consts_in, 16)
            for c in range(4):
                sp.wait_ge(x_in[c], 16)
                sp.wait_ge(feat_in[c], 16)
            for g in range(RAW):
                load_unit(sp, L0, 0, g, True)

            def loads(L):
                for g in range(RAW, NG):
                    load_unit(sp, L, 0, g, False)
                with sp.Fori(1, NB) as b:
                    for g in range(NG):
                        load_unit(sp, L, b, g, False)
                    if L is L1:
                        sp.wait_ge(L1["x_done"], b)
                        sp.dma_start(out_t[:, bass.ds(b * KT - KT, KT), :],
                                     x[:, bass.ds(b * KT - KT, KT), :]).then_inc(out_done, 16)

            def factored0():
                loads(L0)
                for g in range(RAW):
                    sp.wait_ge(L0["q_ready"], NB * NG - RAW + g + 1)
                    load_unit(sp, L1, 0, g, True)

            def general0():
                general_sync(sp, L0)
                for g in range(RAW):
                    load_unit(sp, L1, 0, g, True)

            def factored1():
                loads(L1)
                sp.wait_ge(L1["x_done"], NB)
                sp.dma_start(out_t[:, T - KT:T, :], x[:, T - KT:T, :]).then_inc(out_done, 16)
                sp.wait_ge(out_done, 16 * NB)

            def general1():
                general_sync(sp, L1)
                sp.wait_ge(L1["gen_free"], 2 * T + 1)
                sp.dma_start(out_t[:, :, :], x[:, :, :]).then_inc(out_done, 16)
                sp.wait_ge(out_done, 16)

            branch(sp, L0, factored0, general0)
            sp.wait_ge(fT_ready, 1)
            sp.dma_start(f1_rows, fT[:, :]).then_inc(f1_out, 16)
            sp.wait_ge(f1_out, 16)
            rows = f1_rows.rearrange("(h t) p -> h (t p)", h=2)
            for part, c in enumerate((slice(0, IB), slice(IB, N))):
                for hh in range(2):
                    sp.dma_start(f1bc[hh][:, c], rows[hh, c].partition_broadcast(P)).then_inc(f1_in[part], 16)
            branch(sp, L1, factored1, general1)

        @block.gpsimd
        def _(pool):
            nc.gpsimd.memset(ident[:, :], 0.0).then_inc(ident0, 1)
            nc.gpsimd.memset(A[:, :], 0.0).then_inc(ident0, 1)
            pool.wait_ge(ident0, 2)
            nc.gpsimd.affine_select(out=ident[:, :], in_=ident[:, :], compare_op=ALU.not_equal, fill=1.0, base=0,
                                    pattern=[[-1, P]], channel_multiplier=1).then_inc(ident0, 1)
            for hh in range(2):
                for r in range(2):
                    pool.dma_start(A[64 * hh:64 * hh + 64, 2 * r + hh:2 * r + hh + 1],
                                   a_d[hh, 64 * r:64 * r + 64].unsqueeze(1)).then_inc(A_in, 16)
            nc.gpsimd.memset(mhalf[:, :], -0.5).then_inc(ident0, 1)
            pool.wait_ge(ident0, 4)
            for c in range(4):
                pool_rstd(pool, L0["ln0"], T // 4, c + 1, at=c * T // 4)
            pool_stats(pool, L0, 4)
            with pool.Fori(0, NB) as b:
                pool_rstd(pool, L0["ln1"], KT, b + 1)
            pool_stats(pool, L1, 8)

        @block.scalar
        def _(act):
            for c in range(4):
                act.dma_start(x[:, 8 * c:8 * c + 8, :], x_t[:, 8 * c:8 * c + 8, :]).then_inc(x_in[c], 16)
            act.dma_start(W1, W1_d).then_inc(consts_in, 16)
            act.dma_start(W2, W2_d).then_inc(consts_in, 16)
            act.dma_start(rhs1[:, 0:D], W3T_d).then_inc(consts_in, 16)
            act.dma_start(b3[:, :], pb3_d.partition_broadcast(P)).then_inc(consts_in, 16)
            def apply0(tiles):
                for t in tiles:
                    last = nc.scalar.activation(vals[:, t, 0:D], x[:, t, :], ACT.Relu, bias=nmr[:, t:t + 1],
                                                scale=rstd[:, t:t + 1])
                return last

            for c in range(3):
                act.wait_ge(L0["ln0"]["norm_done"], c + 1)
                apply0(range(c * T // 4, (c + 1) * T // 4)).then_inc(L0["ln0"]["h_done"], 1)
            scalar_weights(act, L0)
            act.wait_ge(L0["ln0"]["norm_done"], 4)

            def f1_chunk(c):
                act.wait_ge(fbc_mm, c + 1)
                nc.scalar.activation(f1bc[0][:, c * IB:(c + 1) * IB], bank[4 + c % 4][:, :], ACT.Identity,
                                     bias=pc[:, 0:1]).then_inc(fbc_ready, 1)

            def split0(g):
                scalar_split(act, L0, g)
                if g < 4:
                    last = apply0(range(3 * T // 4 + 2 * g, 3 * T // 4 + 2 * g + 2))
                    if g == 3:
                        last.then_inc(L0["ln0"]["h_done"], 1)
                f1_chunk(g)
                if g == 7:
                    scalar_vsum(act, L0)

            def first0():
                scalar_signs(L0, 0, 0, True, 0, 2 * G)
                for g in range(1, NG):
                    scalar_unit(act, L0, 0, g, True)

            def factored0():
                scalar_edges(act, L0, 0, 0, True)
                act.wait_ge(L0["e_ready"], 1)
                for g in range(NG):
                    split0(g)
                act.wait_ge(fbc_ready, NB)
                run_core(act, first0, lambda b, g, f: scalar_unit(act, L0, b, g, f), [], [], ())
                for k in range(KT):
                    scalar_evac(act, L0, NB - 1, k)

            def general0():
                apply0(range(3 * T // 4, T)).then_inc(L0["ln0"]["h_done"], 1)
                general_scalar(act, L0)

            branch(act, L0, factored0, general0)
            for c in range(NB):
                act.wait_ge(trans_mm, c + 1)
                nc.scalar.activation(featT[:, c * IB:(c + 1) * IB], bank[c % 2][:, :], ACT.Copy).then_inc(hT_ready, 1)
            scalar_edges(act, L1, 0, 0, True)
            act.wait_ge(ft_mm, 1)
            nc.scalar.activation(fT[:, :], bank[0][0:2 * T, 0:P], ACT.Copy).then_inc(fT_ready, 1)
            scalar_weights(act, L1)

            def first1():
                scalar_split(act, L1, 0)
                rows_of_block0(act)
                scalar_signs(L1, 0, 0, True, 0, 2 * G)
                scalar_split(act, L1, 1)
                for g in range(1, NG):
                    if g + 1 < NG:
                        scalar_split(act, L1, g + 1)
                    scalar_unit(act, L1, 0, g, True)
                    if g == 1:
                        scalar_vsum(act, L1)

            def factored1():
                act.wait_ge(L1["e_ready"], 1)
                run_core(act, first1, lambda b, g, f: scalar_unit(act, L1, b, g, f), [], [], (),
                         lambda: rows_of_others(act))
                for k in range(KT):
                    scalar_evac(act, L1, NB - 1, k)

            branch(act, L1, factored1, lambda: general_scalar(act, L1))

        @block.vector
        def _(dve):
            count = [0]

            def link(ins):
                count[0] += 1
                ins.then_inc(dve_step, 1)
                dve.wait_ge(dve_step, count[0])

            nc.vector.memset(shift[:, 0:1], 4.0)
            nc.vector.memset(shift[:, 1:2], -2.0)
            nc.vector.memset(vals[:, :, D:D + 1], 1.0)
            link(nc.vector.memset(ones[:, :], 1.0))
            dve.wait_ge(first_in, 16 * 4)
            nc.vector.tensor_scalar(bb[:, 0, :], ones[:, :], bcols[:, 0:1], None, ALU.mult).then_inc(bb_ready, 1)
            dve.wait_ge(pv_mm, 1)
            nc.vector.tensor_tensor(pc[:, 0:2], bank[1][:, 0:2], b12[:, :], ALU.add)
            link(nc.vector.tensor_copy(pv[:, 0:2], bank[0][:, 0:2]))
            nc.vector.tensor_scalar(pvb[:, :], ones[:, :], pv[:, 0:1], None, ALU.mult).then_inc(pv_ready, 1)
            for c in range(5):
                if c < 4:
                    dve.wait_ge(x_in[c], 16)
                    nc.vector.memset(pause[:, :], 0.0)
                    ln_stats(L0["ln0"], c, T // 4, at=c * T // 4)
                    ln_mean(dve, L0["ln0"], T // 4, c + 1, at=c * T // 4)
                    ln_var(dve, L0["ln0"], T // 4, c + 1, at=c * T // 4)
                if c >= 1:
                    dve.wait_ge(L0["ln0"]["rstd_done"], c)
                    q4 = slice((c - 1) * T // 4, c * T // 4)
                    nc.vector.scalar_tensor_tensor(out=nmr[:, q4], in0=bag[:, q4, 0], scalar=-1.0, in1=rstd[:, q4],
                                                   op0=ALU.mult, op1=ALU.mult).then_inc(L0["ln0"]["norm_done"], 1)
                if c == 1:
                    dve.wait_ge(consts_in, 16 * 6)
                    dve.wait_ge(A_in, 64)
                    nc.vector.tensor_tensor(w3sq, rhs1[:, 0:D], rhs1[:, 0:D], ALU.mult)
                    for k in (1, 2):
                        last = nc.vector.tensor_scalar(bb[:, k, :], ones[:, :], bcols[:, k:k + 1], None, ALU.mult)
                    last.then_inc(bb_ready, 1)
            dve.wait_ge(pv_ready, 1)
            dve.wait_ge(fcol_mm, 1)
            f0 = bank[2][:, 0:2 * T].rearrange("p (t c) -> p t c", c=2)
            for c in range(2):
                last = nc.vector.tensor_scalar(fc[:, :, c], f0[:, :, c], pc[:, c:c + 1], None, ALU.add)
            last.then_inc(fc_ready, 1)
            dve.wait_ge(fc_ready, 1)
            vector_range(link, L0)
            vector_weights(link, L0)
            vector_flag(link, L0)
            dve.wait_ge(pv_mm, 2)
            nc.vector.tensor_copy(rhs1[:, D:D + 4], bank[0][:, 2:6])
            nc.vector.tensor_copy(pc[:, 2:6], bank[1][:, 2:6])
            nc.vector.tensor_copy(w3n[:, :], bank[3][:, 0:D]).then_inc(pv_ready, 1)
            vector_scale(L0)

            def stats1(b):
                dve.wait_ge(L0["x_done"], b + 1)
                nc.vector.memset(pause[:, :], 0.0)
                ln_stats(L0["ln1"], b, KT)

            def mean1(b):
                ln_mean(dve, L0["ln1"], KT, b + 1)

            def var1(b):
                ln_var(dve, L0["ln1"], KT, b + 1)

            def norm1(b):
                ln_norm(dve, L0["ln1"], b, b + 1)

            def relu1(b):
                ln_relu(dve, L0["ln1"], b, b + 1)

            def core(L, first, more, rest, end):
                steps = [lambda b, step=step: step(dve, L, b) for step in
                         (vector_evac, vector_combine, vector_fix, vector_sum, vector_rden, vector_result)] + more
                at = STEPS_AT[L["i"]]

                def unit(b, g, first):
                    def within():
                        for m in range(len(steps)):
                            if at[m] == g - 0.5:
                                steps[m](b - 1)

                    vector_unit(dve, L, b, g, first, within)

                run_core(dve, first, unit, [lambda b: vector_factors(dve, L, b)], steps, at, rest, end)

            def first0():
                for g in range(NG + LAG):
                    vector_split(dve, L0, g)
                dve.wait_ge(fbc_ready, NB)
                for g in range(NG):
                    vector_unit(dve, L0, 0, g, True)

            def first1():
                for g in range(LAG):
                    vector_split(dve, L1, g)
                for g in range(NG):
                    vector_split(dve, L1, g + LAG)
                    if g == 0:
                        rows_of_block0(dve)
                    if FIRST3[g] == 2:
                        dve.wait_ge(L1["prod_done"], NG)
                        dve.wait_ge(L1["vsum_ready"], 1)
                    vector_unit(dve, L1, 0, g, True)

            v4 = vals3(L1)

            def values1(c):
                dve.wait_ge(v_mm, c + 1)
                nc.vector.memset(v4[:, KT * c:KT * c + KT, :, D // 2:D // 2 + 1], 1.0)
                for half in range(2):
                    t = slice(KT * c + 2 * half, KT * c + 2 * half + 2)
                    src = bank[2 + 2 * (c % 3) + half][:, 0:2 * (D + 4)].rearrange("p (t w) -> p t w", t=2)
                    nc.vector.tensor_tensor(v4[:, t, :, 0:D // 2], src[:, :, 0:D].rearrange("p t (h w) -> p t h w", h=2),
                                            b3[:, :].rearrange("p (o h w) -> p o h w", o=1, h=2).broadcast_to([P, 2, 2, D // 2]),
                                            ALU.add)
                    last = nc.vector.tensor_tensor(fc[:, t, :], src[:, :, D:D + 4],
                                                   pc[:, 2:6].unsqueeze(1).broadcast_to([P, 2, 4]), ALU.add)
                last.then_inc(v_ready, 1)

            def values_bound():
                link(nc.vector.scalar_tensor_tensor(out=vbound[:, 1, :], in0=b3[:, :], scalar=-1.0, in1=b3[:, :],
                                                    op0=ALU.mult, op1=ALU.max))
                link(nc.vector.tensor_scalar(vbound[:, 1, :], vbound[:, 1, :], VMAX, None, ALU.subtract))
                link(nc.vector.tensor_tensor(room, vbound[:, 1, :], vbound[:, 1, :], ALU.mult))
                link(nc.vector.scalar_tensor_tensor(out=vbound[:, 0, :], in0=w3n[:, :], scalar=1.01 * D, in1=room,
                                                    op0=ALU.mult, op1=ALU.subtract))
                link(nc.vector.tensor_reduce(vmax2[:, :], vbound, AX.X, ALU.max))

            def factored0():
                core(L0, first0, [stats1, mean1, var1, norm1, relu1], lambda: None, {8: lambda: (values1(0), values1(1))})

            def general0():
                general_vector(dve, L0)
                with dve.Fori(0, NB) as b:
                    nc.vector.memset(pause[:, :], 0.0)
                    ln_stats(L0["ln1"], b, KT)
                    for step in (mean1, var1, norm1, relu1):
                        step(b)
                values1(0)
                values1(1)

            branch(dve, L0, factored0, general0)

            for c in range(2, NB):
                values1(c)
                if c == 3:
                    values_bound()
            dve.wait_ge(v_ready, NB)
            dve.wait_ge(pv_ready, 2)
            nc.vector.tensor_scalar(ft[:, :, :], fc[:, :, 0:2].rearrange("p t h -> p h t"), 1.0, None,
                                    ALU.mult).then_inc(ft_ready, 1)
            vector_range(link, L1)
            vector_weights(link, L1)
            vector_flag(link, L1)
            vector_scale(L1)

            def factored1():
                core(L1, first1, [], lambda: rows_of_others(dve), {})

            branch(dve, L1, factored1, lambda: general_vector(dve, L1))

        @block.tensor
        def _(pe):
            rhs = (w12[:, :], A[:, 0:2], A[:, 2:4])

            def fold(r, w):
                nc.tensor.matmul(bank[0][:, 2 * r:2 * r + 2], w, rhs[r], start=True, stop=True)
                return nc.tensor.matmul(bank[1][:, 2 * r:2 * r + 2], bb[:, r, :], rhs[r], start=True, stop=True)

            pe.wait_ge(bb_ready, 1)
            fold(0, W).then_inc(pv_mm, 1)
            pe.wait_ge(pv_ready, 1)
            for t in range(T):
                if t % 8 == 0:
                    pe.wait_ge(feat_in[t // 8], 16)
                mm = nc.tensor.matmul(bank[2][:, 2 * t:2 * t + 2], featT[:, t * P:(t + 1) * P], pv[:, 0:2],
                                      start=True, stop=True)
            mm.then_inc(fcol_mm, 1)

            def f1_chunk(c):
                nc.tensor.matmul(bank[4 + c % 4][:, :], pvb[:, :], featT[:, c * IB:(c + 1) * IB],
                                 start=True, stop=True).then_inc(fbc_mm, 1)

            pe.wait_ge(bb_ready, 2)
            fold(1, W1)
            fold(2, W2)
            nc.tensor.matmul(bank[3][:, 0:D], ones[:, :], w3sq, start=True, stop=True).then_inc(pv_mm, 1)
            for c in range(4):
                f1_chunk(c)
            pe.wait_ge(fc_ready, 1)
            pe.wait_ge(pv_ready, 2)

            def factored0():
                for c in range(3):
                    pe.wait_ge(L0["ln0"]["h_done"], c + 1)
                    tensor_vsum(pe, L0, range(c * T // 4, (c + 1) * T // 4))
                for c in range(4, NB):
                    pe.wait_ge(fbc_ready, c - 3)
                    f1_chunk(c)
                pe.wait_ge(L0["ln0"]["h_done"], 4)
                mm = tensor_vsum(pe, L0, range(3 * T // 4, T))
                mm.then_inc(L0["vsum_mm"], 1)
                pe.wait_ge(fbc_ready, NB)
                pe.wait_ge(L0["vsum_ready"], 1)
                tensor_core(pe, L0)
                pe.wait_ge(L0["banks_free"], T - KT + 1)
                transposed(0)
                transposed(1)
                pe.wait_ge(L0["banks_free"], T)

            def general0():
                pe.wait_ge(L0["ln0"]["h_done"], 4)
                general_tensor(pe, L0)
                transposed(0)
                transposed(1)

            def transposed(c):
                pe.wait_ge(L0["ln1"]["h_done"], c + 1)
                if c >= 2:
                    pe.wait_ge(hT_ready, c - 1)
                for j in range(KT):
                    mm = nc.tensor.transpose(bank[c % 2][:, j * P:(j + 1) * P], h[:, KT * c + j, :], ident[:, :])
                mm.then_inc(trans_mm, 1)

            def project(c):
                pe.wait_ge(hT_ready, c + 1)
                if c >= 3:
                    pe.wait_ge(v_ready, c - 2)
                for j in range(KT):
                    t = KT * c + j
                    mm = nc.tensor.matmul(bank[2 + 2 * (c % 3) + j // 2][:, (j % 2) * (D + 4):(j % 2 + 1) * (D + 4)],
                                          featT[:, t * P:(t + 1) * P], rhs1[:, :], start=True, stop=True)
                mm.then_inc(v_mm, 1)

            def factored1():
                tensor_vsum(pe, L1, range(T)).then_inc(L1["vsum_mm"], 1)
                pe.wait_ge(L1["vsum_ready"], 1)
                tensor_core(pe, L1)

            pe.wait_ge(ident0, 4)
            branch(pe, L0, factored0, general0)
            for c in range(NB):
                project(c)
                if c + 2 < NB:
                    transposed(c + 2)
            pe.wait_ge(ft_ready, 1)
            nc.tensor.transpose(bank[0][0:2 * T, 0:P], ft[:, :, :].rearrange("p h t -> p (h t)"), ident[:, :]).then_inc(ft_mm, 1)
            pe.wait_ge(fT_ready, 1)
            pe.wait_ge(v_ready, NB)
            branch(pe, L1, factored1, lambda: general_tensor(pe, L1))


def kernel(x, adj, L0_gnn_inlayer2, L0_gnn_W, L0_gnn_b, L0_gnn_w1, L0_gnn_b1, L0_gnn_w2, L0_gnn_b2,
           L1_gnn_W1, L1_gnn_b1, L1_gnn_W2, L1_gnn_b2, L1_gnn_W3, L1_gnn_b3, L1_gnn_a):
    import numpy as np
    import concourse.bacc as bacc
    from concourse.bass_utils import run_bass_kernel_spmd

    nc = bacc.Bacc("TRN2", target_bir_lowering=False, num_devices=1)
    host = {
        "x": x, "adjT": np.asarray(adj).T, "adj": adj, "inlayer2T": np.asarray(L0_gnn_inlayer2).T,
        "W": L0_gnn_W, "b": L0_gnn_b, "w12": np.stack([np.asarray(L0_gnn_w1), np.asarray(L0_gnn_w2)], axis=1),
        "b12": np.concatenate([np.asarray(L0_gnn_b1), np.asarray(L0_gnn_b2)]),
        "W1": L1_gnn_W1, "W2": L1_gnn_W2, "W3T": np.asarray(L1_gnn_W3).T,
        "pb1": L1_gnn_b1, "pb2": L1_gnn_b2, "pb3": L1_gnn_b3, "a": L1_gnn_a,
    }
    arrays, args = {}, []
    for name, value in host.items():
        value = np.ascontiguousarray(value)
        arrays[f"in_{name}"] = value
        args.append(nc.dram_tensor(f"in_{name}", value.shape, mybir.dt.from_np(value.dtype), kind="ExternalInput").ap())
    args.append(nc.dram_tensor("result", (N, D), F32, kind="ExternalOutput").ap())
    gat_program(nc, *args)
    r = run_bass_kernel_spmd(nc, [arrays], core_ids=[0])
    return r.results[0]["result"]
```
